# Optimizing a Trainium2 kernel written in Bass

```python
import numpy as np
import jax
import jax.numpy as jnp

def _softmax(x, axis=-1):
    return jax.nn.softmax(x, axis=axis)

def _gelu(x):
    return jax.nn.gelu(x, approximate=True)

def _silu(x):
    return jax.nn.silu(x)

def _sigmoid(x):
    return jax.nn.sigmoid(x)

def _layernorm(x, axis=-1, eps=1e-05):
    m = jnp.mean(x, axis=axis, keepdims=True)
    v = jnp.var(x, axis=axis, keepdims=True)
    return (x - m) / jnp.sqrt(v + eps)

def _scatter_add(tgt, idx, src, axis=0):
    return tgt.at[idx].add(src)

def _segment_sum(src, seg, n):
    return jax.ops.segment_sum(src, seg, n)
kernel_name = 'mk_rec_standalone_d1_rec_r8_39ba68'

def setup_inputs(seed: int=0):
    np.random.seed(seed)
    _w = jnp.asarray

    def _rec_inputs():
        import jax
        import jax.numpy as jnp
        _rk = jax.random.key(seed)
        r_user_emb = -0.000608245 + 0.100131 * jax.random.normal(jax.random.fold_in(_rk, 1), (2048, 16), jnp.float32)
        r_seq1_emb = -1.33793e-05 + 0.0999936 * jax.random.normal(jax.random.fold_in(_rk, 2), (2048, 200, 16), jnp.float32)
        r_target1_emb = -0.00064186 + 0.0999588 * jax.random.normal(jax.random.fold_in(_rk, 3), (2048, 16), jnp.float32)
        r_seq2_emb = 9.72762e-06 + 0.100021 * jax.random.normal(jax.random.fold_in(_rk, 4), (2048, 200, 16), jnp.float32)
        r_target2_emb = 0.000458123 + 0.100259 * jax.random.normal(jax.random.fold_in(_rk, 5), (2048, 16), jnp.float32)
        r_seq1_len = jax.random.randint(jax.random.fold_in(_rk, 6), (2048,), 1, 201, jnp.int32)
        r_seq2_len = jax.random.randint(jax.random.fold_in(_rk, 7), (2048,), 1, 201, jnp.int32)
        return (r_user_emb, r_seq1_emb, r_target1_emb, r_seq2_emb, r_target2_emb, r_seq1_len, r_seq2_len)
    r_user_emb, r_seq1_emb, r_target1_emb, r_seq2_emb, r_target2_emb, r_seq1_len, r_seq2_len = _rec_inputs()

    def _L0_rec_setup():
        import jax, jax.numpy as jnp
        import numpy as np
        B, L, D = (512, 200, 16)
        AH1, AH2 = (16, 8)
        MH1, MH2 = (32, 16)

        def dice(x, alpha):
            p = jax.nn.sigmoid(x)
            return p * x + (1.0 - p) * alpha * x

        def din_attention(target, seq, length, p):
            t = jnp.broadcast_to(target[:, None, :], seq.shape)
            inp = jnp.concatenate([t, seq, t - seq, t * seq], axis=-1)
            h = dice(inp @ p['aW1'] + p['ab1'], p['aal1'])
            h = dice(h @ p['aW2'] + p['ab2'], p['aal2'])
            score = (h @ p['aW3'] + p['ab3'])[..., 0]
            mask = jnp.arange(L, dtype=jnp.int32)[None, :] < length[:, None]
            score = jnp.where(mask, score, 0.0)
            return jnp.einsum('bl,bld->bd', score, seq)

        def mlp(x, p):
            h = dice(x @ p['mW1'] + p['mb1'], p['mal1'])
            h = dice(h @ p['mW2'] + p['mb2'], p['mal2'])
            return jax.nn.sigmoid(h @ p['mW3'] + p['mb3'])
        key = jax.random.key(seed)
        ks = jax.random.split(key, 24)
        s = 0.01 ** 0.5
        d = {'user_emb': jax.random.normal(ks[0], (B, D)) * s, 'seq1_emb': jax.random.normal(ks[1], (B, L, D)) * s, 'target1_emb': jax.random.normal(ks[2], (B, D)) * s, 'seq2_emb': jax.random.normal(ks[3], (B, L, D)) * s, 'target2_emb': jax.random.normal(ks[4], (B, D)) * s, 'seq1_len': jax.random.randint(ks[5], (B,), 1, L + 1, dtype=jnp.int32), 'seq2_len': jax.random.randint(ks[6], (B,), 1, L + 1, dtype=jnp.int32), 'aW1': jax.random.normal(ks[7], (4 * D, AH1)) * 0.1, 'ab1': jnp.zeros((AH1,)), 'aal1': jnp.zeros((AH1,)), 'aW2': jax.random.normal(ks[8], (AH1, AH2)) * 0.1, 'ab2': jnp.zeros((AH2,)), 'aal2': jnp.zeros((AH2,)), 'aW3': jax.random.normal(ks[9], (AH2, 1)) * 0.1, 'ab3': jnp.zeros((1,)), 'mW1': jax.random.normal(ks[10], (5 * D, MH1)) * 0.1, 'mb1': jnp.zeros((MH1,)), 'mal1': jnp.zeros((MH1,)), 'mW2': jax.random.normal(ks[11], (MH1, MH2)) * 0.1, 'mb2': jnp.zeros((MH2,)), 'mal2': jnp.zeros((MH2,)), 'mW3': jax.random.normal(ks[12], (MH2, 1)) * 0.1, 'mb3': jnp.zeros((1,))}
        return d
    _L0_rec_all = _L0_rec_setup()
    _L0_rec_in = {k: v for k, v in _L0_rec_all.items() if k in ('aW1', 'ab1', 'aal1', 'aW2', 'ab2', 'aal2', 'aW3', 'ab3', 'mW1', 'mb1', 'mal1', 'mW2', 'mb2', 'mal2', 'mW3', 'mb3')}
    del _L0_rec_all
    return {'r_user_emb': r_user_emb, 'r_seq1_emb': r_seq1_emb, 'r_target1_emb': r_target1_emb, 'r_seq2_emb': r_seq2_emb, 'r_target2_emb': r_target2_emb, 'r_seq1_len': r_seq1_len, 'r_seq2_len': r_seq2_len, 'L0_rec_aW1': _L0_rec_in['aW1'], 'L0_rec_ab1': _L0_rec_in['ab1'], 'L0_rec_aal1': _L0_rec_in['aal1'], 'L0_rec_aW2': _L0_rec_in['aW2'], 'L0_rec_ab2': _L0_rec_in['ab2'], 'L0_rec_aal2': _L0_rec_in['aal2'], 'L0_rec_aW3': _L0_rec_in['aW3'], 'L0_rec_ab3': _L0_rec_in['ab3'], 'L0_rec_mW1': _L0_rec_in['mW1'], 'L0_rec_mb1': _L0_rec_in['mb1'], 'L0_rec_mal1': _L0_rec_in['mal1'], 'L0_rec_mW2': _L0_rec_in['mW2'], 'L0_rec_mb2': _L0_rec_in['mb2'], 'L0_rec_mal2': _L0_rec_in['mal2'], 'L0_rec_mW3': _L0_rec_in['mW3'], 'L0_rec_mb3': _L0_rec_in['mb3']}

def reference(r_user_emb, r_seq1_emb, r_target1_emb, r_seq2_emb, r_target2_emb, r_seq1_len, r_seq2_len, L0_rec_aW1, L0_rec_ab1, L0_rec_aal1, L0_rec_aW2, L0_rec_ab2, L0_rec_aal2, L0_rec_aW3, L0_rec_ab3, L0_rec_mW1, L0_rec_mb1, L0_rec_mal1, L0_rec_mW2, L0_rec_mb2, L0_rec_mal2, L0_rec_mW3, L0_rec_mb3):
    import jax
    import jax.numpy as jnp

    def _L0_rec_ref(user_emb, seq1_emb, target1_emb, seq2_emb, target2_emb, seq1_len, seq2_len, aW1, ab1, aal1, aW2, ab2, aal2, aW3, ab3, mW1, mb1, mal1, mW2, mb2, mal2, mW3, mb3):
        import jax, jax.numpy as jnp
        import numpy as np
        B, L, D = (512, 200, 16)
        AH1, AH2 = (16, 8)
        MH1, MH2 = (32, 16)

        def dice(x, alpha):
            p = jax.nn.sigmoid(x)
            return p * x + (1.0 - p) * alpha * x

        def din_attention(target, seq, length, p):
            t = jnp.broadcast_to(target[:, None, :], seq.shape)
            inp = jnp.concatenate([t, seq, t - seq, t * seq], axis=-1)
            h = dice(inp @ p['aW1'] + p['ab1'], p['aal1'])
            h = dice(h @ p['aW2'] + p['ab2'], p['aal2'])
            score = (h @ p['aW3'] + p['ab3'])[..., 0]
            mask = jnp.arange(L, dtype=jnp.int32)[None, :] < length[:, None]
            score = jnp.where(mask, score, 0.0)
            return jnp.einsum('bl,bld->bd', score, seq)

        def mlp(x, p):
            h = dice(x @ p['mW1'] + p['mb1'], p['mal1'])
            h = dice(h @ p['mW2'] + p['mb2'], p['mal2'])
            return jax.nn.sigmoid(h @ p['mW3'] + p['mb3'])
        p = dict(aW1=aW1, ab1=ab1, aal1=aal1, aW2=aW2, ab2=ab2, aal2=aal2, aW3=aW3, ab3=ab3, mW1=mW1, mb1=mb1, mal1=mal1, mW2=mW2, mb2=mb2, mal2=mal2, mW3=mW3, mb3=mb3)
        pool1 = din_attention(target1_emb, seq1_emb, seq1_len, p)
        pool2 = din_attention(target2_emb, seq2_emb, seq2_len, p)
        emb = jnp.concatenate([user_emb, pool1, target1_emb, pool2, target2_emb], axis=1)
        return mlp(emb, p)
    y = _L0_rec_ref(r_user_emb, r_seq1_emb, r_target1_emb, r_seq2_emb, r_target2_emb, r_seq1_len, r_seq2_len, L0_rec_aW1, L0_rec_ab1, L0_rec_aal1, L0_rec_aW2, L0_rec_ab2, L0_rec_aal2, L0_rec_aW3, L0_rec_ab3, L0_rec_mW1, L0_rec_mb1, L0_rec_mal1, L0_rec_mW2, L0_rec_mb2, L0_rec_mal2, L0_rec_mW3, L0_rec_mb3)
    return y

_drawn_inputs = setup_inputs


def setup_inputs(seed=0):
    import zlib

    import numpy as np

    out = dict(_drawn_inputs(seed))
    spreads = {'L0_rec_ab1': (0.0, 0.8),
     'L0_rec_aal1': (0.0, 0.8),
     'L0_rec_ab2': (0.0, 0.8),
     'L0_rec_aal2': (0.0, 0.8),
     'L0_rec_mb1': (0.0, 0.8),
     'L0_rec_mal1': (0.0, 0.8),
     'L0_rec_mb2': (0.0, 0.8),
     'L0_rec_mal2': (0.0, 0.8)}
    factors = {'r_user_emb': 8.0,
     'r_seq1_emb': 8.0,
     'r_target1_emb': 8.0,
     'r_seq2_emb': 8.0,
     'r_target2_emb': 8.0,
     'L0_rec_aW1': 8.0,
     'L0_rec_aW2': 8.0,
     'L0_rec_aW3': 8.0,
     'L0_rec_mW1': 8.0,
     'L0_rec_mW2': 8.0,
     'L0_rec_mW3': 8.0}
    for name, (base, spread) in spreads.items():
        noise = np.random.default_rng([zlib.crc32(name.encode()), seed]).standard_normal(out[name].shape)
        drawn = base * np.exp(spread * noise) if base else spread * noise
        out[name] = jnp.asarray(drawn.astype(out[name].dtype))
    for name, factor in factors.items():
        out[name] = (out[name] * factor).astype(out[name].dtype)
    return out
```

```python
from contextlib import ExitStack

import numpy as np

import concourse.bass as bass
from concourse import mybir

F32 = mybir.dt.float32
BF16 = mybir.dt.bfloat16
I32 = mybir.dt.int32
ALU = mybir.AluOpType
ACT = mybir.ActivationFunctionType
AX_X = mybir.AxisListType.X

P = 128
B, L, D = 2048, 200, 16
AH1, AH2 = 16, 8
MH1, MH2 = 32, 16
TU = 64
NT = 2 * B // TU
NU, NI = 8, 4
NK = L // NI
KH = NK // 2
KC = 5
UC = NK * NI
COLS = NU * UC
HC = COLS // 2
BC = 2 * UC
SC = NU * KC * NI
RING = 6
PARTS = 3
CK = PARTS * NU
TPAIRS = NT // 2

C_G8 = 0
C_POOL = C_G8 + 8
C_TOK = C_POOL + 32
C_Q4 = C_TOK + NK
C_JT = C_Q4 + 4
C_ID = C_JT + 4
C_W3 = C_ID + P
C_END = C_W3 + KC * P
K_R8, K_R16, K_R32, K_SEL = 0, P, 2 * P, 3 * P
K_END = K_SEL + 4 * P
R_W1, R_W2, R_W3M, R_AL1, R_MB2, R_MAL2 = 0, 64, 72, 73, 74, 75
R_B2, R_AL2, R_W3 = 76, 77, 78
R_MW2, R_MB1, R_MAL1 = 79, 95, 96
R_M1 = 97
R_END = R_M1 + 4 * MH1


def shape_constants():
    p = np.arange(P)
    big = np.zeros((P, C_END), np.float32)
    big[:, C_G8:C_G8 + 8] = p[:, None] // 16 == np.arange(8)
    big[:, C_POOL:C_POOL + 32] = p[:, None] // 4 == np.arange(32)
    big[:, C_TOK:C_TOK + NK] = NK * (p[:, None] % 4) + np.arange(NK)
    big[:, C_Q4:C_Q4 + 4] = p[:, None] // 32 == np.arange(4)
    big[:, C_JT:C_JT + 4] = 2 * (p[:, None] // 64) + (p[:, None] // 16) % 2 == np.arange(4)
    big[:, C_ID:C_ID + P] = np.eye(P)
    w3 = np.zeros((P, KC, P), np.float32)
    for r in range(P):
        half, q, j = r // 64, (r // 16) % 4, (r // 8) % 2
        for kk in range(KC):
            w3[r, kk, 32 * q + 2 * (KC * half + kk) + j] = 1
    big[:, C_W3:] = w3.reshape(P, -1)
    rep = np.zeros((5 * D, K_END), np.float32)
    for at, width in ((K_R8, 8), (K_R16, 16), (K_R32, 32)):
        rep[:width, at:at + P] = np.arange(width)[:, None] == p % width
    for p_ in range(P):
        kh, f = (p_ // 32) % 2, p_ % 16
        rep[(2 * D if kh else 0) + f, K_SEL + p_] = 1
        if kh == 0:
            rep[4 * D + f, K_SEL + P + p_] = 1
        rep[D + f, K_SEL + 2 * P + p_] = 1
        rep[3 * D + f, K_SEL + 3 * P + p_] = 1
    hot = np.zeros((CK, 4, BC), np.float32)
    for k in range(CK):
        u = k % NU
        hot[k, u // 2, (u % 2) * UC:(u % 2 + 1) * UC] = 1
    return big, rep, hot.reshape(CK, -1)


def build(nc, seqs, targets, lens, users, aW1, ab1, aal1, aW2, ab2, aal2, aW3, ab3,
          mW1, mb1, mal1, mW2, mb2, mal2, mW3, mb3, cbig, crep, chot, y_out):
    bias_dram = nc.dram_tensor("bias_parts", (NT, CK * P), BF16).ap()

    with ExitStack() as ctx:
        def sb(name, shape, dt=F32):
            return ctx.enter_context(nc.sbuf_tensor(name, shape, dt))

        def psum(name, shape):
            return ctx.enter_context(nc.psum_tensor(name, shape, F32))

        def sem(name):
            return ctx.enter_context(nc.semaphore(name))

        big = sb("big", [P, C_END])
        rep = sb("rep", [5 * D, K_END])
        hot32 = sb("hot32", [CK, 4 * BC])
        hot = sb("hot", [CK, 4 * BC], BF16)
        small16 = sb("small16", [16, 76])
        small8 = sb("small8", [8, 3])
        small32 = sb("small32", [32, 18])
        mw1 = sb("mw1", [5 * D, MH1])
        b1row = sb("b1row", [1, AH1])
        ones = sb("ones", [1, NT])
        b3col = sb("b3col", [P, 1])
        mb3col = sb("mb3col", [4, 1])
        R = sb("R", [P, R_END])
        oma = sb("oma", [P, 4])
        Ws = sb("Ws", [P, AH1])
        Wc = sb("Wc", [P, AH1])
        BDc = sb("BDc", [P, P])
        BD2 = sb("BD2", [P, 64])
        W3s = sb("W3s", [P, KC * P])
        M1 = sb("M1", [P, 4, P])
        M2 = sb("M2", [P, 64])
        M3 = sb("M3", [64, 4])
        tnat = sb("tnat", [P, 512])
        tT = sb("tT", [P, NT * NU])
        lens_i = sb("lens_i", [P, 32], I32)
        lens4 = sb("lens4", [P, P])
        LN = sb("LN", [P, P])
        Cres = sb("Cres", [NT, NU * P])
        C3 = sb("C3", [NT, PARTS, NU * P], BF16)
        Z = sb("Z", [P, 2, 512])
        ZT = sb("ZT", [P, 2, 512])
        pooled = sb("pooled", [P, NT * D])
        pooledT = sb("pooledT", [P, NT * D])
        X = sb("X", [P, RING, 2 * NK * D])
        cb = sb("cb", [CK, RING, P], BF16)
        XT = sb("XT", [P, 2, COLS])
        W1t = sb("W1t", [P, 2, P])
        W1 = sb("W1", [P, 2, NU, P])
        G1 = sb("G1", [P, 2, 2, BC])
        H1 = sb("H1", [P, 2, COLS])
        G2 = sb("G2", [P, 2, 2, BC])
        H2 = sb("H2", [P, 2, HC])
        SCb = sb("SCb", [P, 2, SC])
        SR = sb("SR", [P, 2, SC])
        MK = sb("MK", [P, 2, 2 * NK], I32)
        SM = sb("SM", [P, 2, 2 * NK])
        PR = sb("PR", [P, 2, 2 * NK * D])
        g1 = sb("g1", [P, 512])
        h1 = sb("h1", [P, 512])
        g2 = sb("g2", [64, 512])
        h2 = sb("h2", [64, 512])
        yt = sb("yt", [4, 512])

        x1 = psum("x1", [P, 4, 512])
        x2 = psum("x2", [P, 2, 512])
        sc = psum("sc", [P, 512])
        pp = psum("pp", [P, 512])

        params_in, targets_in, heads_in = sem("params_in"), sem("targets_in"), sem("heads_in")
        x_in = [sem(f"x_in{r}") for r in range(RING)]
        cb_in = [sem(f"cb_in{r}") for r in range(RING)]
        zeroed, hot_ready, rep_done, rep_ready = sem("zeroed"), sem("hot_ready"), sem("rep_done"), sem("rep_ready")
        lens_ready, ln_done, ln_ready = sem("lens_ready"), sem("ln_done"), sem("ln_ready")
        dve_chain, pool_chain = sem("dve_chain"), sem("pool_chain")
        tT_ready, bdc_ready, c_done, c_split, c_stored = sem("tT_ready"), sem("bdc_ready"), sem("c_done"), sem("c_split"), sem("c_stored")
        w23_ready, m_ready = sem("w23_ready"), sem("m_ready")
        xt_ready, w_ready, l1_done, sig1, gate1, h1_ready = sem("xt_ready"), sem("w_ready"), sem("l1_done"), sem("sig1"), sem("gate1"), sem("h1_ready")
        l2_done, sig2, gate2, h2_ready = sem("l2_done"), sem("sig2"), sem("gate2"), sem("h2_ready")
        l3_done, s_evac, st_done, mk_done, sm_ready = sem("l3_done"), sem("s_evac"), sem("st_done"), sem("mk_done"), sem("sm_ready")
        prod_ready, sum_done, pooled_done = sem("prod_ready"), sem("sum_done"), sem("pooled_done")
        w_mul, w_add = sem("w_mul"), sem("w_add")
        zt_ready, pt_ready, head_mm, head_sig, head_gate, head_h, y_ready, y_stored = (
            sem(n) for n in ("zt_ready", "pt_ready", "head_mm", "head_sig", "head_gate", "head_h", "y_ready", "y_stored"))

        N_PARAMS, N_TARGETS, N_HEADS = 16, 8, 3 * 2
        tok = big[:, C_TOK:C_TOK + NK]
        FIRST, LAST = -1, NT + 4
        LOOP0 = 5
        LOOPS = (NT - 1 - LOOP0) // RING
        LOOP1 = LOOP0 + LOOPS * RING

        def run_slots(eng, step):
            for s in range(FIRST, LOOP0):
                step(s, s)
            with eng.Fori(0, LOOPS) as n:
                for d in range(RING):
                    step(n * RING + (LOOP0 + d), LOOP0 + d, n)
            for s in range(LOOP1, LAST):
                step(s, s)

        def tile(slot, known, rnd, lag):
            return rnd is not None or 0 <= known - lag < NT, slot - lag, known - lag

        def tiles_before(t, known, rnd, n):
            return rnd is not None or known >= n

        def loads(known, rnd):
            done = 16 * (known // RING + 1)
            return done if rnd is None else rnd * 16 + done

        block = ctx.enter_context(nc.Block())

        @block.sync
        def _(sp):
            def load_x(t, r):
                sp.dma_start(X[:, r, :].rearrange("p (j c) -> p j c", j=2),
                             seqs[bass.ds(t, 1), :, :, :].rearrange("o j p c -> p (o j) c")).then_inc(x_in[r], 16)

            def load_bias(t, r):
                sp.dma_start(cb[:, r, :], bias_dram[bass.ds(t, 1), :].rearrange("o (k m) -> (o k) m", m=P)
                             ).then_inc(cb_in[r], 16)

            load_x(0, 0)
            tv = targets.rearrange("(th tl j q u) f -> q j tl u th f", tl=4, j=2, q=4, u=8)
            for q in range(4):
                for j in range(2):
                    for tl in range(4):
                        at = 32 * q + 8 * tl
                        sp.dma_start(tnat[at:at + 8, :].rearrange("p (th j f) -> p th j f", j=2, f=D)[:, :, j, :],
                                     tv[q, j, tl]).then_inc(targets_in, 16)
            for t in range(1, RING):
                load_x(t, t)
            sp.wait_ge(c_split, PARTS)
            sp.dma_start(bias_dram[:, :], C3[:].rearrange("t a m -> t (a m)")).then_inc(c_stored, 16)
            sp.wait_ge(c_stored, 16)
            for t in range(RING):
                load_bias(t, t)
            uv = users.rearrange("(t j u) f -> j u t f", j=2, u=32)
            tg = targets.rearrange("(s t j u) f -> s j u t f", s=2, j=2, u=32)
            for j in range(2):
                for at, n, src in ((64 * j, 0, uv[j]), (64 * j + 32, 0, tg[0, j]), (64 * j, 1, tg[1, j])):
                    sp.dma_start(Z[at:at + 32, n, :].rearrange("p (t f) -> p t f", f=D), src).then_inc(heads_in, 16)

            def load(t, r):
                sp.wait_ge(prod_ready, t - (RING - 1))
                load_x(t, r)
                load_bias(t, r)

            rounds = (NT - RING) // RING
            with sp.Fori(0, rounds) as n:
                for r in range(RING):
                    load(n * RING + (RING + r), r)
            for t in range(RING * (rounds + 1), NT):
                load(t, t % RING)
            sp.wait_ge(y_ready, 1)
            sp.dma_start(y_out.rearrange("(tp p j u) o -> p j tp (u o)", p=2, j=2, u=32)[0, 0],
                         yt[0:1, :].rearrange("p (t u) -> p t u", u=32)).then_inc(y_stored, 16)
            for c in range(1, 4):
                sp.dma_start(y_out.rearrange("(tp p j u) o -> p j tp (u o)", p=2, j=2, u=32)[c % 2, c // 2],
                             yt[c:c + 1, :].rearrange("p (t u) -> p t u", u=32)).then_inc(y_stored, 16)
            sp.wait_ge(y_stored, 64)

        @block.scalar
        def _(act):
            act.dma_start(rep[:], crep).then_inc(params_in, 16)
            act.dma_start(small16[:, 0:64].rearrange("f (m h) -> f m h", h=AH1),
                          aW1.rearrange("(m f) h -> f m h", f=D)).then_inc(params_in, 16)
            act.dma_start(small16[:, 64:72], aW2).then_inc(params_in, 16)
            act.dma_start(small16[:, 72:73], mW3).then_inc(params_in, 16)
            for n, v in enumerate((aal1, mb2, mal2)):
                act.dma_start(small16[:, 73 + n:74 + n], v[:, None]).then_inc(params_in, 16)
            for n, v in enumerate((ab2[:, None], aal2[:, None], aW3)):
                act.dma_start(small8[:, n:n + 1], v).then_inc(params_in, 16)
            act.dma_start(small32[:, 0:16], mW2).then_inc(params_in, 16)
            for n, v in enumerate((mb1, mal1)):
                act.dma_start(small32[:, 16 + n:17 + n], v[:, None]).then_inc(params_in, 16)
            act.dma_start(mw1[:], mW1).then_inc(params_in, 16)
            act.dma_start(b1row[:], ab1[None, :]).then_inc(params_in, 16)
            act.dma_start(big[:], cbig).then_inc(params_in, 16)
            act.dma_start(lens_i[:], lens).then_inc(targets_in, 16)
            act.dma_start(b3col[:], ab3[None, :].to_broadcast([P, 1])).then_inc(heads_in, 16)
            act.dma_start(mb3col[:], mb3[None, :].to_broadcast([4, 1])).then_inc(heads_in, 16)
            act.dma_start(hot32[:], chot).then_inc(targets_in, 16)
            act.wait_ge(heads_in, 16 * (N_HEADS + 2))
            act.wait_ge(rep_ready, 2)

            def step(slot, known, rnd=None):
                runs, t, k = tile(slot, known, rnd, 3)
                if runs:
                    act.wait_ge(l3_done, t + 1)
                    if tiles_before(t, k, rnd, 2):
                        act.wait_ge(st_done, t - 1)
                    nc.scalar.activation(SCb[:, k % 2, :].rearrange("p (k u i) -> p k u i", u=NU, i=NI),
                                         sc[:, 0:SC].rearrange("p (u k i) -> p k u i", u=NU, i=NI),
                                         ACT.Identity, bias=b3col[:, 0:1]).then_inc(s_evac, 1)
                runs, t, k = tile(slot, known, rnd, 0)
                if runs:
                    for a in range(2):
                        act.wait_ge(l1_done, 2 * t + (a + 1))
                        nc.scalar.activation(G1[:, a], x1[:, 2 * a:2 * a + 2, 0:BC], ACT.Sigmoid).then_inc(sig1, 1)
                        act.wait_ge(sig1, 2 * t + (a + 1))
                        nc.scalar.activation(G1[:, a], G1[:, a], ACT.Identity, bias=R[:, R_AL1:R_AL1 + 1],
                                             scale=oma[:, 0:1]).then_inc(gate1, 1)
                runs, t, k = tile(slot, known, rnd, 1)
                if runs:
                    act.wait_ge(l2_done, t + 1)
                    if tiles_before(t, k, rnd, 2):
                        act.wait_ge(h2_ready, t - 1)
                    nc.scalar.activation(G2[:, k % 2], x2[:, :, 0:BC], ACT.Sigmoid,
                                         bias=R[:, R_B2:R_B2 + 1]).then_inc(sig2, 1)
                    act.wait_ge(sig2, t + 1)
                    nc.scalar.activation(G2[:, k % 2], G2[:, k % 2], ACT.Identity, bias=R[:, R_AL2:R_AL2 + 1],
                                         scale=oma[:, 1:2]).then_inc(gate2, 1)

            run_slots(act, step)
            act.wait_ge(head_mm, 1)
            nc.scalar.activation(g1[:], x1[:, 0, :], ACT.Sigmoid, bias=R[:, R_MB1:R_MB1 + 1]).then_inc(head_sig, 1)
            act.wait_ge(head_mm, 2)
            nc.scalar.activation(g2[:], x1[0:64, 1, :], ACT.Sigmoid, bias=R[0:64, R_MB2:R_MB2 + 1]).then_inc(head_sig, 1)
            act.wait_ge(head_mm, 3)
            nc.scalar.activation(yt[:], x1[0:4, 2, :], ACT.Sigmoid, bias=mb3col[:, 0:1]).then_inc(y_ready, 1)

        @block.vector
        def _(dve):
            count = [0]

            def chain(ins):
                count[0] += 1
                ins.then_inc(dve_chain, 1)
                dve.wait_ge(dve_chain, count[0])

            nc.vector.memset(ones[:], 1.0).then_inc(zeroed, 1)
            nc.vector.memset(Z[32:64, 1, :], 0.0).then_inc(zeroed, 1)
            nc.vector.memset(Z[96:128, 1, :], 0.0).then_inc(zeroed, 1)
            dve.wait_ge(rep_done, 1)
            nc.vector.tensor_copy(R[:], x2[:, 0, 0:R_END]).then_inc(rep_ready, 1)
            dve.wait_ge(rep_ready, 1)
            dve.wait_ge(params_in, 16 * N_PARAMS)
            w1m = [R[:, R_W1 + m * AH1:R_W1 + (m + 1) * AH1] for m in range(4)]
            chain(nc.vector.tensor_tensor(Wc[:], w1m[0], w1m[2], ALU.add))
            nc.vector.tensor_tensor(BDc[:].rearrange("p (g h) -> p g h", g=8),
                                    big[:, C_G8:C_G8 + 8].unsqueeze(2).to_broadcast([P, 8, AH1]),
                                    Wc[:].unsqueeze(1).to_broadcast([P, 8, AH1]), ALU.mult).then_inc(bdc_ready, 1)
            chain(nc.vector.tensor_tensor(Ws[:], w1m[1], w1m[2], ALU.subtract))
            dve.wait_ge(targets_in, 16 * (32 + 2))
            nc.vector.transpose(tT[:], tnat[:]).then_inc(tT_ready, 1)
            for n, (at) in enumerate((R_AL1, R_AL2, R_MAL1, R_MAL2)):
                chain(nc.vector.tensor_scalar(oma[:, n:n + 1], R[:, at:at + 1], -1.0, 1.0, ALU.mult, ALU.add))
            nc.vector.tensor_tensor(BD2[:].rearrange("p (g h) -> p g h", g=8),
                                    big[:, C_G8:C_G8 + 8].unsqueeze(2).to_broadcast([P, 8, AH2]),
                                    R[:, R_W2:R_W2 + AH2].unsqueeze(1).to_broadcast([P, 8, AH2]),
                                    ALU.mult).then_inc(rep_ready, 1)
            nc.vector.tensor_copy(lens4[:].rearrange("p (u i) -> p u i", i=4),
                                  lens_i[:].unsqueeze(2).to_broadcast([P, 32, 4])).then_inc(lens_ready, 1)
            nc.vector.tensor_scalar(W3s[:], big[:, C_W3:C_END], R[:, R_W3:R_W3 + 1], None,
                                    ALU.mult).then_inc(w23_ready, 1)
            dve.wait_ge(c_done, 1)
            c_ps = x1[0:NT, 0:2, :].rearrange("p b c -> p (b c)")
            nc.vector.tensor_copy(C3[:, 0, :], c_ps).then_inc(c_split, 1)
            dve.wait_ge(c_split, 1)
            chain(nc.vector.tensor_tensor(Cres[:], c_ps, C3[:, 0, :], ALU.subtract))
            nc.vector.tensor_copy(C3[:, 1, :], Cres[:]).then_inc(c_split, 1)
            dve.wait_ge(c_split, 2)
            chain(nc.vector.tensor_tensor(Cres[:], Cres[:], C3[:, 1, :], ALU.subtract))
            nc.vector.tensor_copy(C3[:, 2, :], Cres[:]).then_inc(c_split, 1)
            dve.wait_ge(ln_done, 1)
            nc.vector.tensor_copy(LN[:], x2[:, 1, 0:P]).then_inc(ln_ready, 1)
            dve.wait_ge(ln_ready, 1)

            def step(slot, known, rnd=None):
                runs, t, k = tile(slot, known, rnd, -1)
                if runs:
                    dve.wait_ge(x_in[k % RING], loads(k, rnd))
                    if tiles_before(t, k, rnd, 2):
                        dve.wait_ge(l1_done, 2 * t - 2)
                    nc.vector.transpose(
                        XT[:, k % 2, :].rearrange("p (u k i) -> p k u i", u=NU, i=NI),
                        X[:, k % RING, :].rearrange("p (j k f) -> p k j f", j=2, f=D)).then_inc(xt_ready, 1)
                runs, t, k = tile(slot, known, rnd, 3)
                if runs:
                    dve.wait_ge(s_evac, t + 1)
                    if tiles_before(t, k, rnd, 2):
                        dve.wait_ge(sm_ready, t - 1)
                    nc.vector.transpose(SR[:, k % 2, :], SCb[:, k % 2, :]).then_inc(st_done, 1)
                    for j in range(2):
                        nc.vector.tensor_scalar(MK[:, k % 2, j * NK:(j + 1) * NK], tok, LN[:, bass.ds(t * 2 + j, 1)],
                                                -1.0, ALU.is_lt, ALU.mult).then_inc(mk_done, 1)
                    dve.wait_ge(st_done, t + 1)
                    dve.wait_ge(mk_done, 2 * t + 2)
                    nc.vector.tensor_tensor(
                        SM[:, k % 2, :].bitcast(I32).rearrange("p (j m k) -> p j m k", j=2, k=KC),
                        MK[:, k % 2, :].rearrange("p (j m k) -> p j m k", j=2, k=KC),
                        SR[:, k % 2, :].bitcast(I32).rearrange("p (k m j) -> p j m k", k=KC, j=2)[:, :, 0:2 * KC, :],
                        ALU.bitwise_and).then_inc(sm_ready, 1)
                runs, t, k = tile(slot, known, rnd, 4)
                if runs:
                    dve.wait_ge(sum_done, t + 1)
                    nc.vector.reduce_sum(pooled[:, bass.ds(t * D, D)],
                                         pp[:, 0:KH * D].rearrange("p (k f) -> p f k", f=D),
                                         AX_X).then_inc(pooled_done, 1)
                runs, t, k = tile(slot, known, rnd, 0)
                if runs:
                    for a in range(2):
                        dve.wait_ge(gate1, 2 * t + (a + 1))
                        if a == 0 and tiles_before(t, k, rnd, 2):
                            dve.wait_ge(l2_done, t - 1)
                        nc.vector.tensor_tensor(
                            H1[:, k % 2, a * HC:(a + 1) * HC].rearrange("p (b c) -> p b c", b=2),
                            G1[:, a], x1[:, 2 * a:2 * a + 2, 0:BC], ALU.mult).then_inc(h1_ready, 1)
                runs, t, k = tile(slot, known, rnd, 1)
                if runs:
                    dve.wait_ge(gate2, t + 1)
                    if tiles_before(t, k, rnd, 2):
                        dve.wait_ge(l3_done, t - 1)
                    nc.vector.scalar_tensor_tensor(
                        out=H2[:, k % 2, :].rearrange("p (b c) -> p b c", b=2), in0=x2[:, :, 0:BC],
                        scalar=R[:, R_B2:R_B2 + 1], in1=G2[:, k % 2], op0=ALU.add, op1=ALU.mult).then_inc(h2_ready, 1)

            run_slots(dve, step)
            dve.wait_ge(heads_in, 16 * (N_HEADS + 2))
            dve.wait_ge(zeroed, 3)
            for n in range(2):
                nc.vector.transpose(ZT[:, n, :], Z[:, n, :]).then_inc(zt_ready, 1)
            dve.wait_ge(pooled_done, NT)
            nc.vector.transpose(pooledT[:], pooled[:]).then_inc(pt_ready, 1)
            dve.wait_ge(head_sig, 1)
            chain(nc.vector.tensor_scalar(g1[:], g1[:], oma[:, 2:3], R[:, R_MAL1:R_MAL1 + 1], ALU.mult, ALU.add))
            nc.vector.scalar_tensor_tensor(out=h1[:], in0=x1[:, 0, :], scalar=R[:, R_MB1:R_MB1 + 1], in1=g1[:],
                                           op0=ALU.add, op1=ALU.mult).then_inc(head_h, 1)
            dve.wait_ge(head_sig, 2)
            chain(nc.vector.tensor_scalar(g2[:], g2[:], oma[0:64, 3:4], R[0:64, R_MAL2:R_MAL2 + 1],
                                          ALU.mult, ALU.add))
            nc.vector.scalar_tensor_tensor(out=h2[:], in0=x1[0:64, 1, :], scalar=R[0:64, R_MB2:R_MB2 + 1],
                                           in1=g2[:], op0=ALU.add, op1=ALU.mult).then_inc(head_h, 1)

        @block.gpsimd
        def _(pool):
            pool.wait_ge(targets_in, 16 * (32 + 2))
            nc.gpsimd.tensor_copy(hot[:], hot32[:]).then_inc(hot_ready, 1)
            pool.wait_ge(hot_ready, 1)
            pool.wait_ge(rep_ready, 2)
            pool.wait_ge(tT_ready, 1)

            def step(slot, known, rnd=None):
                runs, t, k = tile(slot, known, rnd, -1)
                if runs:
                    if tiles_before(t, k, rnd, 1):
                        pool.wait_ge(w_ready, t)
                    nc.gpsimd.tensor_tensor(
                        W1t[:, 0, :].rearrange("p (u h) -> p u h", u=NU),
                        R[:, R_W1 + 3 * AH1:R_W1 + 4 * AH1].unsqueeze(1).to_broadcast([P, NU, AH1]),
                        tT[:, bass.ds(t * NU, NU)].unsqueeze(2).to_broadcast([P, NU, AH1]),
                        ALU.mult).then_inc(w_mul, 1)
                    pool.wait_ge(w_mul, t + 1)
                    nc.gpsimd.tensor_tensor(
                        W1t[:, 1, :].rearrange("p (u h) -> p u h", u=NU), W1t[:, 0, :].rearrange("p (u h) -> p u h", u=NU),
                        Ws[:].unsqueeze(1).to_broadcast([P, NU, AH1]), ALU.add).then_inc(w_add, 1)
                    pool.wait_ge(w_add, t + 1)
                    if tiles_before(t, k, rnd, 2):
                        pool.wait_ge(l1_done, 2 * t - 2)
                    nc.gpsimd.tensor_tensor(
                        W1[:, k % 2].rearrange("p u (g h) -> p u g h", g=8),
                        W1t[:, 1, :].rearrange("p (u h) -> p u h", u=NU).unsqueeze(2).to_broadcast([P, NU, 8, AH1]),
                        big[:, C_G8:C_G8 + 8].unsqueeze(1).unsqueeze(3).to_broadcast([P, NU, 8, AH1]),
                        ALU.mult).then_inc(w_ready, 1)
                if known == 0 and rnd is None:
                    for n in range(4):
                        nc.gpsimd.tensor_tensor(
                            M1[:, n, :].rearrange("p (c h) -> p c h", c=4),
                            R[:, R_M1 + n * MH1:R_M1 + (n + 1) * MH1].unsqueeze(1).to_broadcast([P, 4, MH1]),
                            big[:, C_JT:C_JT + 4].unsqueeze(2).to_broadcast([P, 4, MH1]), ALU.mult).then_inc(m_ready, 1)
                    nc.gpsimd.tensor_tensor(
                        M2[:].rearrange("p (c h) -> p c h", c=4),
                        R[:, R_MW2:R_MW2 + MH2].unsqueeze(1).to_broadcast([P, 4, MH2]),
                        big[:, C_Q4:C_Q4 + 4].unsqueeze(2).to_broadcast([P, 4, MH2]), ALU.mult).then_inc(m_ready, 1)
                    nc.gpsimd.tensor_scalar(M3[:], big[0:64, C_G8:C_G8 + 4], R[0:64, R_W3M:R_W3M + 1], None,
                                            ALU.mult).then_inc(m_ready, 1)
                runs, t, k = tile(slot, known, rnd, 3)
                if runs:
                    pool.wait_ge(sm_ready, t + 1)
                    if tiles_before(t, k, rnd, 2):
                        pool.wait_ge(sum_done, t - 1)
                    nc.gpsimd.tensor_tensor(
                        PR[:, k % 2, :].rearrange("p (c f) -> p c f", f=D), X[:, k % RING, :].rearrange("p (c f) -> p c f", f=D),
                        SM[:, k % 2, :].unsqueeze(2).to_broadcast([P, 2 * NK, D]), ALU.mult).then_inc(prod_ready, 1)

            run_slots(pool, step)

        @block.tensor
        def _(pe):
            pe.wait_ge(params_in, 16 * N_PARAMS)
            mm = nc.tensor.matmul
            mm(x2[:, 0, 0:76], rep[0:16, K_R16:K_R16 + P], small16[:], start=True, stop=True)
            mm(x2[:, 0, 76:79], rep[0:8, K_R8:K_R8 + P], small8[:], start=True, stop=True)
            mm(x2[:, 0, 79:97], rep[0:32, K_R32:K_R32 + P], small32[:], start=True, stop=True)
            for n in range(4):
                last = mm(x2[:, 0, R_M1 + n * MH1:R_M1 + (n + 1) * MH1], rep[:, K_SEL + n * P:K_SEL + (n + 1) * P],
                          mw1[:], start=True, stop=True)
            last.then_inc(rep_done, 1)
            pe.wait_ge(zeroed, 1)
            pe.wait_ge(bdc_ready, 1)
            pe.wait_ge(tT_ready, 1)
            for bank in range(2):
                mm(x1[0:NT, bank, :].rearrange("p (s h) -> p s h", h=AH1), ones[:],
                   b1row[:].unsqueeze(1).to_broadcast([1, 32, AH1]), start=True, stop=False)
                for u in range(4 * bank, 4 * bank + 4):
                    last = mm(x1[0:NT, bank, (u % 4) * P:(u % 4 + 1) * P],
                              tT[:].rearrange("p (t u) -> p u t", u=NU)[:, u, :], BDc[:], start=False, stop=u % 4 == 3)
            last.then_inc(c_done, 1)
            pe.wait_ge(lens_ready, 1)
            mm(x2[:, 1, 0:P], lens4[:], big[:, C_ID:C_ID + P], start=True, stop=True).then_inc(ln_done, 1)
            pe.wait_ge(w23_ready, 1)
            pe.wait_ge(ln_ready, 1)
            pe.wait_ge(hot_ready, 1)
            pe.wait_ge(c_split, PARTS)

            def step(slot, known, rnd=None):
                runs, t, k = tile(slot, known, rnd, 0)
                if runs:
                    for a in range(2):
                        if a == 0:
                            pe.wait_ge(cb_in[k % RING], loads(k, rnd))
                            pe.wait_ge(xt_ready, t + 1)
                            pe.wait_ge(w_ready, t + 1)
                        if tiles_before(t, k, rnd, 1):
                            pe.wait_ge(h1_ready, 2 * t + (a - 1))
                        for bank in (2 * a, 2 * a + 1):
                            mm(x1[:, bank, 0:BC], cb[:, k % RING, :], hot[:, bank * BC:(bank + 1) * BC],
                               start=True, stop=False)
                            for u in (2 * bank, 2 * bank + 1):
                                last = mm(x1[:, bank, (u % 2) * UC:(u % 2 + 1) * UC], W1[:, k % 2, u, :],
                                          XT[:, k % 2, u * UC:(u + 1) * UC], start=False, stop=u % 2 == 1)
                        last.then_inc(l1_done, 1)
                runs, t, k = tile(slot, known, rnd, 1)
                if runs:
                    pe.wait_ge(h1_ready, 2 * t + 2)
                    if tiles_before(t, k, rnd, 1):
                        pe.wait_ge(h2_ready, t)
                    hv = H1[:, k % 2, :].rearrange("p (u c) -> p u c", u=NU)
                    for v in range(2):
                        for half in range(2):
                            last = mm(x2[64 * half:64 * half + 64, v, 0:BC].rearrange("p (u c) -> p u c", u=4), BD2[:],
                                      hv[:, 4 * v:4 * v + 4, half * KH * NI:(half + 1) * KH * NI], start=True, stop=True)
                    last.then_inc(l2_done, 1)
                runs, t, k = tile(slot, known, rnd, 2)
                if runs:
                    pe.wait_ge(h2_ready, t + 1)
                    if tiles_before(t, k, rnd, 1):
                        pe.wait_ge(s_evac, t)
                    hv = H2[:, k % 2, :].rearrange("p (u k c) -> p k u c", u=NU, k=KC)
                    for kk in range(KC):
                        last = mm(sc[:, 0:SC].rearrange("p (u c) -> p u c", u=NU), W3s[:, kk * P:(kk + 1) * P],
                                  hv[:, kk], start=kk == 0, stop=kk == KC - 1)
                    last.then_inc(l3_done, 1)
                runs, t, k = tile(slot, known, rnd, 3)
                if runs:
                    pe.wait_ge(prod_ready, t + 1)
                    if tiles_before(t, k, rnd, 1):
                        pe.wait_ge(pooled_done, t)
                    for c in range(4):
                        last = mm(pp[32 * c:32 * c + 32, 0:KH * D], big[:, C_POOL:C_POOL + 32],
                                  PR[:, k % 2, c * KH * D:(c + 1) * KH * D], start=True, stop=True)
                    last.then_inc(sum_done, 1)

            run_slots(pe, step)
            pe.wait_ge(m_ready, 6)
            pe.wait_ge(zt_ready, 2)
            for n in range(2):
                mm(x1[:, 0, :], M1[:, n, :], ZT[:, n, :], start=n == 0, stop=False)
            pe.wait_ge(pt_ready, 1)
            for n in range(2):
                last = mm(x1[:, 0, :], M1[:, 2 + n, :], pooledT[:, n * 512:(n + 1) * 512], start=False, stop=n == 1)
            last.then_inc(head_mm, 1)
            pe.wait_ge(head_h, 1)
            mm(x1[0:64, 1, :], M2[:], h1[:], start=True, stop=True).then_inc(head_mm, 1)
            pe.wait_ge(head_h, 2)
            mm(x1[0:4, 2, :], M3[:], h2[:], start=True, stop=True).then_inc(head_mm, 1)


def kernel(**inputs):
    import concourse.bacc as bacc
    from concourse.bass_utils import run_bass_kernel_spmd

    a = {k.removeprefix("L0_rec_"): np.asarray(v) for k, v in inputs.items()}
    big, rep, hot = shape_constants()
    arrays = {
        "seqs": np.concatenate([a["r_seq1_emb"], a["r_seq2_emb"]]).reshape(NT, 2, P, NK * D),
        "targets": np.concatenate([a["r_target1_emb"], a["r_target2_emb"]]),
        "lens": np.concatenate([a["r_seq1_len"], a["r_seq2_len"]]).reshape(P, 32),
        "users": a["r_user_emb"],
    }
    for name in ("aW1", "ab1", "aal1", "aW2", "ab2", "aal2", "aW3", "ab3",
                 "mW1", "mb1", "mal1", "mW2", "mb2", "mal2", "mW3", "mb3"):
        arrays[name] = a[name]
    arrays |= {"cbig": big, "crep": rep, "chot": hot}
    arrays = {k: np.ascontiguousarray(v) for k, v in arrays.items()}

    nc = bacc.Bacc("TRN2", target_bir_lowering=False, num_devices=1)
    args = [nc.dram_tensor(f"in_{k}", v.shape, mybir.dt.from_np(v.dtype), kind="ExternalInput").ap()
            for k, v in arrays.items()]
    y = nc.dram_tensor("y", (B, 1), F32, kind="ExternalOutput").ap()
    build(nc, *args, y)
    r = run_bass_kernel_spmd(nc, [{f"in_{k}": v for k, v in arrays.items()}], core_ids=[0])
    return r.results[0]["y"]
```

```python
from contextlib import ExitStack

import numpy as np

import concourse.bass as bass
from concourse import mybir

F32 = mybir.dt.float32
BF16 = mybir.dt.bfloat16
I32 = mybir.dt.int32
U16 = mybir.dt.uint16
ALU = mybir.AluOpType
ACT = mybir.ActivationFunctionType
AX_X = mybir.AxisListType.X

P = 128
B, L, D = 2048, 200, 16
AH1, AH2 = 16, 8
MH1, MH2 = 32, 16
TU = 64
NT = 2 * B // TU
NU, NI, NA = 8, 4, 2
NK = L // (NA * NI)
NC = 4
KC = -(-NK // NC)
K_OF = [0, KC, 2 * KC, NK - KC]
QJ = 8
UC = L
COLS = NU * UC
HC = COLS // 2
BC = 2 * UC
SC = KC * NU * NI
TS = NA * KC * QJ
RING = 3
UNROLL = 6
SUMMED = NT - 4
PARTS = 3
CK = PARTS * NU

C_G8 = 0
C_POOL = C_G8 + 8
C_TOK = C_POOL + 4 * 32
C_Q4 = C_TOK + NA * KC
C_JT = C_Q4 + 4
C_W3 = C_JT + 4
C_END = C_W3 + 32
K_R1, K_R8, K_R16, K_R32, K_SEL = 0, P, 2 * P, 3 * P, 4 * P
K_ONE8 = K_SEL + 3 * P
K_W32 = K_ONE8 + P
K_W16A = K_W32 + MH2 + 2
K_W8 = K_W16A + 2
K_W16B = K_W8 + 3
K_MW1 = K_W16B + 4 * AH1 + AH2 + 2
K_B3 = K_MW1 + MH1
K_B1 = K_B3 + 2
K_END = K_B1 + AH1
R_W1 = 0
R_W2 = R_W1 + 4 * AH1
R_W3M, R_MB2 = R_W2 + AH2, R_W2 + AH2 + 1
R_B1 = R_MB2 + 1
R_EARLY = R_B1 + AH1
R_MW2, R_MB1 = R_EARLY, R_EARLY + MH2
R_AL = R_MB1 + 1
R_B2, R_W3 = R_AL + 4, R_AL + 5
R_M1 = R_W3 + 1
R_B3, R_MB3 = R_M1 + 3 * MH1, R_M1 + 3 * MH1 + 1
R_END = R_MB3 + 1
A_M1, A_1, A_M2, A_2 = range(4)


def shape_constants():
    p = np.arange(P)
    big = np.zeros((P, C_END), np.float32)
    big[:, C_G8:C_G8 + 8] = p[:, None] // 16 == np.arange(8)
    for q in range(4):
        big[:, C_POOL + 32 * q:C_POOL + 32 * q + 32] = 8 * q + (p[:, None] // NI) % NU == np.arange(32)
    kk = np.arange(KC)
    for c in range(NC):
        double = K_OF[c] + kk < (K_OF[c - 1] + KC if c else 0)
        for i in range(NI):
            at = np.concatenate([np.where(double, 2 * L, L // NA * a + NI * (K_OF[c] + kk) + i) for a in range(NA)])
            big[p[(p // 32 == c) & (p % NI == i)], C_TOK:C_TOK + NA * KC] = at
    big[:, C_Q4:C_Q4 + 4] = p[:, None] // 32 == np.arange(4)
    big[:, C_JT:C_JT + 4] = 2 * (p[:, None] // 64) + (p[:, None] // 16) % 2 == np.arange(4)
    big[:, C_W3:] = p[:, None] // 8 == np.arange(32)
    rep = np.zeros((5 * D, K_W32), np.float32)
    rep[:8, K_ONE8:] = 1
    for at, width in ((K_R1, 1), (K_R8, 8), (K_R16, 16), (K_R32, 32)):
        rep[:width, at:at + P] = np.arange(width)[:, None] == p % width
    for p_ in range(P):
        h, f = (p_ // 32) % 2, p_ % 16
        rep[(2 * D if h else 0) + f, K_SEL + p_] = 1
        if h == 0:
            rep[4 * D + f, K_SEL + P + p_] = 1
        rep[(3 * D if h else D) + f, K_SEL + 2 * P + p_] = 1
    hot = np.zeros((CK, 4, BC), np.float32)
    for k in range(CK):
        u = 2 * (k % (NU // 2)) + k // (CK // 2)
        hot[k, u // 2, (u % 2) * UC:(u % 2 + 1) * UC] = 1
    hot_bits = hot.reshape(CK, -1).astype(np.uint16) * np.uint16(0x3F80)
    return big, rep, hot_bits


def build(nc, tokens_t, tokens_r, targets, lens, heads, params, cbig, chot, y_out):
    bias_dram = nc.dram_tensor("bias_parts", (NT, CK * P), BF16).ap()

    with ExitStack() as ctx:
        def sb(name, shape, dt=F32):
            return ctx.enter_context(nc.sbuf_tensor(name, shape, dt))

        def psum(name, shape):
            return ctx.enter_context(nc.psum_tensor(name, shape, F32))

        def sem(name):
            return ctx.enter_context(nc.semaphore(name))

        big = sb("big", [P, C_END])
        par = sb("par", [5 * D, K_END])
        hot = sb("hot", [CK, 4 * BC], BF16)
        R = sb("R", [P, R_END])
        beta = sb("beta", [P, 4])
        is_one = sb("is_one", [P, 4])
        ratio = sb("ratio", [P, 4])
        inv_beta = sb("inv_beta", [P, 4])
        oma = sb("oma", [P, 4])
        w3beta = sb("w3beta", [P, 1])
        w2beta = sb("w2beta", [P, AH2])
        w3ab = sb("w3ab", [8, 2])
        Ws = sb("Ws", [P, AH1])
        Wc = sb("Wc", [P, AH1])
        BDc = sb("BDc", [P, P])
        BD2 = sb("BD2", [P, 64])
        W3s = sb("W3s", [P, 32])
        M1 = sb("M1", [P, 3, P])
        M2 = sb("M2", [P, 64])
        M3 = sb("M3", [64, 4])
        tT = sb("tT", [P, NT * NU])
        lens_i = sb("lens_i", [P, NT * QJ], I32)
        LN = sb("LN", [P, NT * QJ])
        Cres = sb("Cres", [P, NU // 2 * P])
        C3 = sb("C3", [P, PARTS, NU // 2 * P], BF16)
        ZT = sb("ZT", [P, 2, 512])
        pooled = sb("pooled", [P, NT * QJ * D])
        pools = sb("pools", [P, 512])
        poolsT = sb("poolsT", [P, 512])
        X = sb("X", [P, RING, TS * D])
        XT = sb("XT", [P, RING, COLS])
        cb = sb("cb", [CK, RING, P], BF16)
        W1t = sb("W1t", [P, 2, P])
        W1c = sb("W1c", [P, 2, P])
        W1 = sb("W1", [P, 2, NU, P])
        G1 = sb("G1", [P, 2, 2 * BC])
        H1 = sb("H1", [P, 2, COLS])
        G2 = sb("G2", [P, 2, 2, BC])
        H2 = sb("H2", [P, 2, HC])
        SCb = sb("SCb", [P, 2, SC])
        SR = sb("SR", [P, 2, SC])
        MK = sb("MK", [P, NT * TS], I32)
        SM = sb("SM", [P, 2, TS])
        PR = sb("PR", [P, 2, TS * D])
        PF = sb("PF", [P, 2, TS * D // 2])
        g1, g2 = G1[:, 0, 0:512], G1[0:64, 1, 0:512]
        h1, h2 = H1[:, 0, 0:512], H1[0:64, 1, 0:512]
        yt = sb("yt", [4, 512])

        x1 = psum("x1", [P, 4, 512])
        x2 = psum("x2", [P, 2, 512])
        sc = psum("sc", [P, 512])
        pp = psum("pp", [P, 512])

        params_in, targets_in, heads_in, big_in, hot_in, lens_in = (
            sem(n) for n in ("params_in", "targets_in", "heads_in", "big_in", "hot_in", "lens_in"))
        x_in = [sem(f"x_in{r}") for r in range(RING)]
        xt_in = [sem(f"xt_in{r}") for r in range(RING)]
        first_cb = [sem(f"first_cb{r}") for r in range(RING)]
        cb_in = [sem(f"cb_in{r}") for r in range(RING)]
        rep_done, rep_ready, par_ready = sem("rep_done"), sem("rep_ready"), sem("par_ready")
        dve_chain = sem("dve_chain")
        bdc_ready, c_done, c_split, c_stored = sem("bdc_ready"), sem("c_done"), sem("c_split"), sem("c_stored")
        w23_ready, m_ready = sem("w23_ready"), sem("m_ready")
        w_ready, l1_done, silu1_ready, h1_ready = sem("w_ready"), sem("l1_done"), sem("silu1_ready"), sem("h1_ready")
        l2_done, silu2_ready, h2_ready = sem("l2_done"), sem("silu2_ready"), sem("h2_ready")
        l3_done, s_evac, st_done, ln_ready, mk_diff, mk_done, sm_ready = sem("l3_done"), sem("s_evac"), sem("st_done"), sem("ln_ready"), sem("mk_diff"), sem("mk_done"), sem("sm_ready")
        prod_ready, pooled_done = sem("prod_ready"), sem("pooled_done")
        w_mul, w_add = sem("w_mul"), sem("w_add")
        fold_ready, w3ab_ready = sem("fold_ready"), sem("w3ab_ready")
        sum_done, pools_ready, pt_ready, head_mm, head_sig, head_gate, head_h, y_ready, y_stored = (
            sem(n) for n in ("sum_done", "pools_ready", "pt_ready", "head_mm", "head_sig", "head_gate", "head_h", "y_ready", "y_stored"))

        positions = big[:, C_TOK:C_TOK + NA * KC]
        FIRST, LAST = -2, NT + 4
        LOOP0 = 5
        LOOPS = (NT - 2 - LOOP0) // UNROLL
        LOOP1 = LOOP0 + LOOPS * UNROLL

        def run_slots(eng, step):
            for s in range(FIRST, LOOP0):
                step(s, s)
            with eng.Fori(0, LOOPS) as n:
                for d in range(UNROLL):
                    step(n * UNROLL + (LOOP0 + d), LOOP0 + d, n)
            for s in range(LOOP1, LAST):
                step(s, s)

        def tile(slot, known, rnd, lag):
            return rnd is not None or 0 <= known - lag < NT, slot - lag, known - lag

        def tiles_before(t, known, rnd, n):
            return rnd is not None or known >= n

        def loads(known, rnd):
            done = 16 * (known // RING + 1)
            return done if rnd is None else rnd * (16 * UNROLL // RING) + done

        block = ctx.enter_context(nc.Block())

        @block.sync
        def _(sp):
            def load_t(t, r):
                sp.dma_start(XT[:, r, :], tokens_t[bass.ds(t, 1), :, :].rearrange("o p c -> (o p) c")).then_inc(xt_in[r], 16)

            def load_r(t, r):
                sp.dma_start(X[:, r, :], tokens_r[bass.ds(t, 1), :, :].rearrange("o p c -> (o p) c")).then_inc(x_in[r], 16)

            def load_bias(t, r):
                sp.dma_start(cb[:, r, :], bias_dram[bass.ds(t, 1), :].rearrange("o (k m) -> (o k) m", m=P)
                             ).then_inc(cb_in[r], 16)

            sp.dma_start(tT[:], targets).then_inc(targets_in, 16)
            sp.dma_start(lens_i[:], lens).then_inc(lens_in, 16)
            for t in range(2):
                load_t(t, t)
            sp.wait_ge(c_split, PARTS)
            for t in range(RING):
                for u in range(2):
                    sp.dma_start(cb[u * CK // 2:(u + 1) * CK // 2, t, :],
                                 C3[2 * t + u:2 * t + u + 1].rearrange("p a (v m) -> p (a v) m", m=P)).then_inc(first_cb[t], 16)
            sp.dma_start(bias_dram.rearrange("t (v c) -> (t v) c", v=2), C3[:].rearrange("p a m -> p (a m)")).then_inc(c_stored, 16)
            sp.wait_ge(c_stored, 16)
            load_t(2, 2)

            def load(t, k):
                if k < NT:
                    sp.wait_ge(l1_done, 2 * t - (2 * RING - 2))
                    load_t(t, k % RING)
                    load_bias(t, k % RING)
                if k >= 2 * RING:
                    sp.wait_ge(prod_ready, t - (2 * RING - 1))
                load_r(t - RING, k % RING)

            rounds = (NT - 2 * RING) // RING
            for t in range(RING, 2 * RING):
                load(t, t)
                if t == RING:
                    sp.dma_start(ZT[:].rearrange("p n c -> p (n c)"), heads).then_inc(heads_in, 16)
            with sp.Fori(0, rounds) as n:
                for r in range(RING):
                    load(n * RING + (2 * RING + r), 2 * RING + r)
            for t in range(RING * (rounds + 2), NT + RING):
                load(t, t)
            sp.wait_ge(y_ready, 1)
            sp.dma_start(y_out, yt[:]).then_inc(y_stored, 16)
            sp.wait_ge(y_stored, 16)

        @block.scalar
        def _(act):
            act.dma_start(par[:], params).then_inc(params_in, 16)
            act.dma_start(big[:], cbig).then_inc(big_in, 16)
            act.dma_start(hot[:].bitcast(U16), chot).then_inc(hot_in, 16)
            act.wait_ge(big_in, 16)
            def expand(t, k, g):
                nc.scalar.activation(
                    W1[:, k % 2, :, g * AH1:(g + 1) * AH1],
                    W1c[:, k % 2, :].rearrange("p (u h) -> p u h", u=NU),
                    ACT.Identity, scale=big[:, C_G8 + g:C_G8 + g + 1]).then_inc(w_ready, 1)

            for t in range(2):
                act.wait_ge(w_add, t + 1)
                for g in range(8):
                    expand(t, t, g)
            act.wait_ge(rep_ready, 2)

            def step(slot, known, rnd=None):
                runs, t, k = tile(slot, known, rnd, 3)
                if runs:
                    act.wait_ge(l3_done, t + 1)
                    if tiles_before(t, k, rnd, 2):
                        act.wait_ge(st_done, t - 1)
                    nc.scalar.activation(SCb[:, k % 2, :], sc[:, 0:SC], ACT.Identity, bias=R[:, R_B3:R_B3 + 1]).then_inc(s_evac, 1)
                for a in range(2):
                    runs, t, k = tile(slot, known, rnd, 0)
                    if runs:
                        act.wait_ge(l1_done, 2 * t + (a + 1))
                        nc.scalar.activation(G1[:, a].rearrange("p (b c) -> p b c", b=2), x1[:, 2 * a:2 * a + 2, 0:BC],
                                             ACT.Silu).then_inc(silu1_ready, 1)
                    runs, t, k = tile(slot, known, rnd, -1)
                    if a == 0 and runs and (rnd is not None or k >= 2):
                        act.wait_ge(w_add, t + 1)
                        if tiles_before(t, k, rnd, 2):
                            act.wait_ge(l1_done, 2 * t - 2)
                        for g in range(8):
                            expand(t, k, g)
                runs, t, k = tile(slot, known, rnd, 1)
                if runs:
                    act.wait_ge(l2_done, t + 1)
                    if tiles_before(t, k, rnd, 2):
                        act.wait_ge(h2_ready, t - 1)
                    nc.scalar.activation(G2[:, k % 2], x2[:, :, 0:BC], ACT.Silu,
                                         bias=R[:, R_B2:R_B2 + 1]).then_inc(silu2_ready, 1)

            run_slots(act, step)
            act.wait_ge(head_mm, 1)
            nc.scalar.activation(g1, x1[:, 0, :], ACT.Sigmoid, bias=R[:, R_MB1:R_MB1 + 1]).then_inc(head_sig, 1)
            act.wait_ge(head_mm, 2)
            nc.scalar.activation(g2, x1[0:64, 1, :], ACT.Sigmoid, bias=R[0:64, R_MB2:R_MB2 + 1]).then_inc(head_sig, 1)
            act.wait_ge(head_mm, 3)
            nc.scalar.activation(yt[:], x1[0:4, 2, :], ACT.Sigmoid, bias=R[0:4, R_MB3:R_MB3 + 1]).then_inc(y_ready, 1)

        @block.vector
        def _(dve):
            count = [0]

            def chain(ins):
                count[0] += 1
                ins.then_inc(dve_chain, 1)
                dve.wait_ge(dve_chain, count[0])

            def user_weights(t, k):
                nc.vector.tensor_tensor(
                    W1t[:, k % 2, :].rearrange("p (v u h) -> p v u h", u=2, h=AH1),
                    R[:, R_W1 + 3 * AH1:R_W1 + 4 * AH1].unsqueeze(1).unsqueeze(1).to_broadcast([P, NU // 2, 2, AH1]),
                    tT[:].rearrange("p (v tu) -> p v tu", v=NU // 2)[:, :, bass.ds(t * 2, 2)].unsqueeze(3)
                    .to_broadcast([P, NU // 2, 2, AH1]),
                    ALU.mult).then_inc(w_mul, 1)
                dve.wait_ge(w_mul, t + 1)
                nc.vector.tensor_tensor(
                    W1c[:, k % 2, :].rearrange("p (u h) -> p u h", u=NU),
                    W1t[:, k % 2, :].rearrange("p (u h) -> p u h", u=NU),
                    Ws[:].unsqueeze(1).to_broadcast([P, NU, AH1]), ALU.add).then_inc(w_add, 1)

            dve.wait_ge(rep_done, 1)
            nc.vector.tensor_copy(R[:, 0:R_EARLY], x2[:, 0, 0:R_EARLY]).then_inc(rep_ready, 1)
            dve.wait_ge(rep_ready, 1)
            w1m = [R[:, R_W1 + m * AH1:R_W1 + (m + 1) * AH1] for m in range(4)]
            chain(nc.vector.tensor_tensor(Wc[:], w1m[0], w1m[2], ALU.add))
            dve.wait_ge(big_in, 16)
            nc.vector.tensor_tensor(BDc[:].rearrange("p (g h) -> p g h", g=8),
                                    big[:, C_G8:C_G8 + 8].unsqueeze(2).to_broadcast([P, 8, AH1]),
                                    Wc[:].unsqueeze(1).to_broadcast([P, 8, AH1]), ALU.mult).then_inc(bdc_ready, 1)
            chain(nc.vector.tensor_tensor(Ws[:], w1m[1], w1m[2], ALU.subtract))
            dve.wait_ge(targets_in, 16)
            for t in range(2):
                user_weights(t, t)
            dve.wait_ge(lens_in, 16)
            nc.vector.tensor_copy(LN[:], lens_i[:]).then_inc(ln_ready, 1)
            dve.wait_ge(c_done, 1)
            chain(nc.vector.tensor_tensor(
                Cres[:].rearrange("p (s h) -> p s h", h=AH1), x1[:, 0, :].rearrange("p (s h) -> p s h", h=AH1),
                R[:, R_B1:R_B1 + AH1].unsqueeze(1).to_broadcast([P, 32, AH1]), ALU.add))
            for n in range(PARTS):
                nc.vector.tensor_copy(C3[:, n, :], Cres[:]).then_inc(c_split, 1)
                if n < PARTS - 1:
                    dve.wait_ge(c_split, n + 1)
                    chain(nc.vector.tensor_tensor(Cres[:], Cres[:], C3[:, n, :], ALU.subtract))
            w8 = par[0:8, K_W8:K_W8 + 3]
            chain(nc.vector.tensor_tensor(w3ab[:, 0:1], w8[:, 2:3], w8[:, 0:1], ALU.mult))
            nc.vector.tensor_tensor(w3ab[:, 1:2], w3ab[:, 0:1], w8[:, 1:2], ALU.mult).then_inc(w3ab_ready, 1)
            dve.wait_ge(rep_done, 2)
            nc.vector.tensor_copy(R[:, R_EARLY:R_END], x2[:, 1, R_EARLY:R_END]).then_inc(rep_ready, 1)
            dve.wait_ge(rep_ready, 2)
            alphas = R[:, R_AL:R_AL + 4]
            chain(nc.vector.tensor_scalar(oma[:], alphas, -1.0, 1.0, ALU.mult, ALU.add))
            chain(nc.vector.tensor_scalar(is_one[:], oma[:], 0.0, 2.0 ** -30, ALU.is_equal, ALU.mult))
            chain(nc.vector.tensor_tensor(beta[:], oma[:], is_one[:], ALU.add))
            chain(nc.vector.reciprocal(inv_beta[:], beta[:]))
            chain(nc.vector.tensor_tensor(ratio[:], alphas, inv_beta[:], ALU.mult))
            chain(nc.vector.tensor_scalar(w2beta[:], R[:, R_W2:R_W2 + AH2], beta[:, A_1:A_1 + 1], None, ALU.mult))
            nc.vector.tensor_tensor(BD2[:].rearrange("p (g h) -> p g h", g=8),
                                    big[:, C_G8:C_G8 + 8].unsqueeze(2).to_broadcast([P, 8, AH2]),
                                    w2beta[:].unsqueeze(1).to_broadcast([P, 8, AH2]),
                                    ALU.mult).then_inc(par_ready, 1)
            chain(nc.vector.tensor_scalar(w3beta[:], R[:, R_W3:R_W3 + 1], beta[:, A_2:A_2 + 1], None, ALU.mult))
            nc.vector.tensor_scalar(W3s[:], big[:, C_W3:C_END], w3beta[:, 0:1], None,
                                    ALU.mult).then_inc(par_ready, 1)

            def masks(n):
                span = slice(n * NT // 2 * TS, (n + 1) * NT // 2 * TS)
                dve.wait_ge(mk_diff, n + 1)
                nc.vector.tensor_scalar(MK[:, span], MK[:, span].bitcast(F32), 0.0, -1.0, ALU.is_lt,
                                        ALU.mult).then_inc(mk_done, 1)

            masks(0)

            def step(slot, known, rnd=None):
                if known == 1 and rnd is None:
                    masks(1)
                runs, t, k = tile(slot, known, rnd, 3)
                if runs:
                    dve.wait_ge(s_evac, t + 1)
                    if tiles_before(t, k, rnd, 2):
                        dve.wait_ge(sm_ready, t - 1)
                    nc.vector.transpose(SR[:, k % 2, :], SCb[:, k % 2, :]).then_inc(st_done, 1)
                    if rnd is None and k == 0:
                        dve.wait_ge(mk_done, 2)
                    dve.wait_ge(st_done, t + 1)
                    if tiles_before(t, k, rnd, 2):
                        dve.wait_ge(prod_ready, t - 1)
                    nc.vector.tensor_tensor(
                        SM[:, k % 2, :].bitcast(I32).rearrange("p (a k r) -> p a k r", a=NA, k=KC),
                        MK[:, bass.ds(t * TS, TS)].rearrange("p (a k r) -> p a k r", a=NA, k=KC),
                        SR[:, k % 2, :].bitcast(I32).rearrange("p (k b r) -> p b k r", k=KC, r=QJ)[:, 0:NA],
                        ALU.bitwise_and).then_inc(sm_ready, 1)
                runs, t, k = tile(slot, known, rnd, 4)
                if runs:
                    dve.wait_ge(fold_ready, t + 1)
                    nc.vector.reduce_sum(pooled[:, bass.ds(t * (QJ * D), QJ * D)],
                                         PF[:, k % 2].rearrange("p (k c) -> p c k", k=KC), AX_X).then_inc(pooled_done, 1)
                runs, t, k = tile(slot, known, rnd, -2)
                if runs and (rnd is not None or k >= 2):
                    dve.wait_ge(w_ready, 8 * t - 8)
                    user_weights(t, k)
                runs, t, k = tile(slot, known, rnd, 0)
                if runs:
                    for a in range(2):
                        dve.wait_ge(silu1_ready, 2 * t + (a + 1))
                        if a == 0 and tiles_before(t, k, rnd, 2):
                            dve.wait_ge(l2_done, t - 1)
                        nc.vector.scalar_tensor_tensor(
                            out=H1[:, k % 2, a * HC:(a + 1) * HC].rearrange("p (b c) -> p b c", b=2),
                            in0=x1[:, 2 * a:2 * a + 2, 0:BC], scalar=ratio[:, A_1:A_1 + 1], in1=G1[:, a].rearrange("p (b c) -> p b c", b=2),
                            op0=ALU.mult, op1=ALU.add).then_inc(h1_ready, 1)
                runs, t, k = tile(slot, known, rnd, 1)
                if runs:
                    dve.wait_ge(silu2_ready, t + 1)
                    if tiles_before(t, k, rnd, 2):
                        dve.wait_ge(l3_done, t - 1)
                    nc.vector.scalar_tensor_tensor(
                        out=H2[:, k % 2, :].rearrange("p (b c) -> p b c", b=2), in0=x2[:, :, 0:BC],
                        scalar=ratio[:, A_2:A_2 + 1], in1=G2[:, k % 2], op0=ALU.mult, op1=ALU.add).then_inc(h2_ready, 1)

            run_slots(dve, step)
            dve.wait_ge(sum_done, 2)
            nc.vector.tensor_copy(pools[:], pp[:]).then_inc(pools_ready, 1)
            dve.wait_ge(pools_ready, 1)
            nc.vector.transpose(poolsT[:], pools[:]).then_inc(pt_ready, 1)
            dve.wait_ge(head_sig, 1)
            chain(nc.vector.tensor_scalar(g1, g1, oma[:, A_M1:A_M1 + 1], R[:, R_AL + A_M1:R_AL + A_M1 + 1], ALU.mult, ALU.add))
            nc.vector.scalar_tensor_tensor(out=h1, in0=x1[:, 0, :], scalar=R[:, R_MB1:R_MB1 + 1], in1=g1,
                                           op0=ALU.add, op1=ALU.mult).then_inc(head_h, 1)
            dve.wait_ge(head_sig, 2)
            chain(nc.vector.tensor_scalar(g2, g2, oma[0:64, A_M2:A_M2 + 1], R[0:64, R_AL + A_M2:R_AL + A_M2 + 1],
                                          ALU.mult, ALU.add))
            nc.vector.scalar_tensor_tensor(out=h2, in0=x1[0:64, 1, :], scalar=R[0:64, R_MB2:R_MB2 + 1],
                                           in1=g2, op0=ALU.add, op1=ALU.mult).then_inc(head_h, 1)

        @block.gpsimd
        def _(pool):
            pool.wait_ge(big_in, 16)
            pool.wait_ge(ln_ready, 1)
            for n in range(2):
                nc.gpsimd.tensor_tensor(
                    MK[:, n * NT // 2 * TS:(n + 1) * NT // 2 * TS].bitcast(F32).rearrange("p (t a r) -> p t a r", t=NT // 2, r=QJ),
                    positions.unsqueeze(1).unsqueeze(3).to_broadcast([P, NT // 2, NA * KC, QJ]),
                    LN[:, n * NT // 2 * QJ:(n + 1) * NT // 2 * QJ].rearrange("p (t r) -> p t r", r=QJ).unsqueeze(2)
                    .to_broadcast([P, NT // 2, NA * KC, QJ]), ALU.subtract).then_inc(mk_diff, 1)

            def step(slot, known, rnd=None):
                if known == 0 and rnd is None:
                    pool.wait_ge(rep_ready, 2)
                    for n in range(3):
                        nc.gpsimd.tensor_tensor(
                            M1[:, n, :].rearrange("p (c h) -> p c h", c=4),
                            R[:, R_M1 + n * MH1:R_M1 + (n + 1) * MH1].unsqueeze(1).to_broadcast([P, 4, MH1]),
                            big[:, C_JT:C_JT + 4].unsqueeze(2).to_broadcast([P, 4, MH1]), ALU.mult).then_inc(m_ready, 1)
                    nc.gpsimd.tensor_tensor(
                        M2[:].rearrange("p (c h) -> p c h", c=4),
                        R[:, R_MW2:R_MW2 + MH2].unsqueeze(1).to_broadcast([P, 4, MH2]),
                        big[:, C_Q4:C_Q4 + 4].unsqueeze(2).to_broadcast([P, 4, MH2]), ALU.mult).then_inc(m_ready, 1)
                    nc.gpsimd.tensor_scalar(M3[:], big[0:64, C_G8:C_G8 + 4], R[0:64, R_W3M:R_W3M + 1], None,
                                            ALU.mult).then_inc(m_ready, 1)
                runs, t, k = tile(slot, known, rnd, 3)
                if runs:
                    pool.wait_ge(x_in[k % RING], loads(k, rnd))
                    pool.wait_ge(sm_ready, t + 1)
                    if tiles_before(t, k, rnd, 2):
                        pool.wait_ge(fold_ready, t - 1)
                    nc.gpsimd.tensor_tensor(
                        PR[:, k % 2, :].rearrange("p (c f) -> p c f", f=D), X[:, k % RING, :].rearrange("p (c f) -> p c f", f=D),
                        SM[:, k % 2, :].unsqueeze(2).to_broadcast([P, TS, D]), ALU.mult).then_inc(prod_ready, 1)
                    pool.wait_ge(prod_ready, t + 1)
                    if tiles_before(t, k, rnd, 2):
                        pool.wait_ge(pooled_done, t - 1)
                    nc.gpsimd.tensor_tensor(PF[:, k % 2], PR[:, k % 2, 0:TS * D // 2], PR[:, k % 2, TS * D // 2:],
                                            ALU.add).then_inc(fold_ready, 1)

            run_slots(pool, step)

        @block.tensor
        def _(pe):
            pe.wait_ge(params_in, 16)
            mm = nc.tensor.matmul
            def spread(bank, at, rows, which, lo, hi, **flags):
                return mm(x2[:, bank, at:at + hi - lo], par[0:rows, which:which + P], par[0:rows, lo:hi], **flags)

            whole = dict(start=True, stop=True)
            spread(0, R_W1, 16, K_R16, K_W16B, K_MW1, **whole)
            spread(0, R_B1, 1, K_R1, K_B1, K_END, **whole).then_inc(rep_done, 1)
            pe.wait_ge(targets_in, 16)
            pe.wait_ge(bdc_ready, 1)
            for v in range(NU // 2):
                last = mm(x1[:, 0, v * P:(v + 1) * P], tT[:, v * P:(v + 1) * P], BDc[:], **whole)
            last.then_inc(c_done, 1)
            spread(1, R_MW2, 32, K_R32, K_W32, K_W16A, **whole)
            spread(1, R_AL + 1, 16, K_R16, K_W16A, K_W8, **whole)
            spread(1, R_AL + 3, 8, K_R8, K_W8, K_W16B, **whole)
            for n in range(3):
                spread(1, R_M1 + n * MH1, 5 * D, K_SEL + n * P, K_MW1, K_MW1 + MH1, **whole)
            spread(1, R_B3, 1, K_R1, K_B3, K_B3 + 2, start=True, stop=False)
            pe.wait_ge(w3ab_ready, 1)
            mm(x2[:, 1, R_B3:R_B3 + 1], par[0:8, K_ONE8:K_ONE8 + P], w3ab[:, 1:2], start=False,
               stop=True).then_inc(rep_done, 1)
            pe.wait_ge(par_ready, 2)
            pe.wait_ge(hot_in, 16)
            pe.wait_ge(c_split, 1)

            def step(slot, known, rnd=None):
                runs, t, k = tile(slot, known, rnd, 0)
                if runs:
                    for a in range(2):
                        if a == 0:
                            if rnd is None and k < RING:
                                pe.wait_ge(first_cb[k], 32)
                            else:
                                pe.wait_ge(cb_in[k % RING], loads(k - RING, rnd))
                            pe.wait_ge(xt_in[k % RING], loads(k, rnd))
                            pe.wait_ge(w_ready, 8 * t + 8)
                        if tiles_before(t, k, rnd, 1):
                            pe.wait_ge(h1_ready, 2 * t + (a - 1))
                        for bank in (2 * a, 2 * a + 1):
                            mm(x1[:, bank, 0:BC], cb[:, k % RING, :], hot[:, bank * BC:(bank + 1) * BC],
                               start=True, stop=False)
                            for u in (2 * bank, 2 * bank + 1):
                                last = mm(x1[:, bank, (u % 2) * UC:(u % 2 + 1) * UC], W1[:, k % 2, u, :],
                                          XT[:, k % RING, u * UC:(u + 1) * UC], start=False, stop=u % 2 == 1)
                        last.then_inc(l1_done, 1)
                runs, t, k = tile(slot, known, rnd, 1)
                if runs:
                    pe.wait_ge(h1_ready, 2 * t + 2)
                    if tiles_before(t, k, rnd, 1):
                        pe.wait_ge(h2_ready, t)
                    hv = H1[:, k % 2, :].rearrange("p (u c) -> p u c", u=NU)
                    for v in range(2):
                        for half in range(2):
                            last = mm(x2[64 * half:64 * half + 64, v, 0:BC].rearrange("p (u c) -> p u c", u=4), BD2[:],
                                      hv[:, 4 * v:4 * v + 4, half * UC // 2:(half + 1) * UC // 2], start=True, stop=True)
                    last.then_inc(l2_done, 1)
                runs, t, k = tile(slot, known, rnd, 2)
                if runs:
                    pe.wait_ge(h2_ready, t + 1)
                    if tiles_before(t, k, rnd, 1):
                        pe.wait_ge(s_evac, t)
                    hv = H2[:, k % 2, :].rearrange("p (u k i) -> p k u i", u=NU, i=NI)
                    for c in range(NC):
                        last = mm(sc[32 * c:32 * c + 32, 0:SC].rearrange("p (k u i) -> p k u i", u=NU, i=NI), W3s[:],
                                  hv[:, K_OF[c]:K_OF[c] + KC], start=True, stop=True)
                    last.then_inc(l3_done, 1)
                if rnd is None and known == NT + 1:
                    pe.wait_ge(h1_ready, 2 * NT)
                    pe.wait_ge(m_ready, 5)
                    pe.wait_ge(heads_in, 16)
                    for n in range(2):
                        mm(x1[:, 0, :], M1[:, n, :], ZT[:, n, :], start=n == 0, stop=False)

                    pool_sums(0, SUMMED)

            def pool_sums(lo, hi):
                pe.wait_ge(pooled_done, hi)
                pv = pooled[:].rearrange("p (s t q j f) -> p s j q t f", s=2, q=4, j=2, f=D)
                for q in range(4):
                    for s in range(2):
                        t0, t1 = max(lo - s * NT // 2, 0), min(hi - s * NT // 2, NT // 2)
                        for j in range(2 if t0 < t1 else 0):
                            c = 2 * j + s
                            last = mm(pp[32 * c:32 * c + 32, t0 * D:t1 * D].rearrange("p (t f) -> p t f", f=D),
                                      big[:, C_POOL + 32 * q:C_POOL + 32 * q + 32], pv[:, s, j, q, t0:t1],
                                      start=q == 0, stop=q == 3)
                last.then_inc(sum_done, 1)

            run_slots(pe, step)
            pool_sums(SUMMED, NT)
            pe.wait_ge(pt_ready, 1)
            mm(x1[:, 0, :], M1[:, 2, :], poolsT[:], start=False, stop=True).then_inc(head_mm, 1)
            pe.wait_ge(head_h, 1)
            mm(x1[0:64, 1, :], M2[:], h1, start=True, stop=True).then_inc(head_mm, 1)
            pe.wait_ge(head_h, 2)
            mm(x1[0:4, 2, :], M3[:], h2, start=True, stop=True).then_inc(head_mm, 1)


def kernel(**inputs):
    import concourse.bacc as bacc
    from concourse.bass_utils import run_bass_kernel_spmd

    a = {k.removeprefix("L0_rec_"): np.asarray(v) for k, v in inputs.items()}
    big, rep, hot = shape_constants()
    params = np.zeros((5 * D, K_END), np.float32)
    params[:, :K_W32] = rep
    w1 = a["aW1"].reshape(4, D, AH1)

    def put(at, *columns):
        for c in columns:
            c = c.reshape(len(c), -1)
            params[:len(c), at:at + c.shape[1]] = c
            at += c.shape[1]

    put(K_W32, a["mW2"], a["mb1"], a["mal1"])
    put(K_W16A, a["aal1"], a["mal2"])
    put(K_W8, a["aal2"], a["ab2"], a["aW3"])
    put(K_W16B, *w1, a["aW2"], a["mW3"], a["mb2"])
    put(K_MW1, a["mW1"])
    put(K_B1, a["ab1"][None])
    put(K_B3, a["ab3"], a["mb3"])
    targets = np.concatenate([a["r_target1_emb"], a["r_target2_emb"]])
    lens = np.concatenate([a["r_seq1_len"], a["r_seq2_len"]])
    heads = np.zeros((2, 2, 32, 2, NT // 2, D), np.float32)
    of_tile = [v.reshape(NT // 2, 2, 32, D).transpose(1, 2, 0, 3)
               for v in (a["r_user_emb"], a["r_target1_emb"], a["r_target2_emb"])]
    heads[:, 0, :, 0], heads[:, 1, :, 0], heads[:, 0, :, 1] = of_tile
    tokens = np.concatenate([a["r_seq1_emb"], a["r_seq2_emb"]]).reshape(NT, 2, 4, NU, NA, NK, NI, D)
    tokens_r = np.zeros((NT, NC, NU, NI, NA, KC, 4, 2, D), np.float32)
    for c in range(NC):
        doubles = K_OF[c - 1] + KC - K_OF[c] if c else 0
        tokens_r[:, c, :, :, :, doubles:] = tokens[..., K_OF[c] + doubles:K_OF[c] + KC, :, :].transpose(0, 3, 6, 4, 5, 2, 1, 7)
    arrays = {
        "tokens_t": tokens.transpose(0, 2, 1, 7, 3, 4, 5, 6).reshape(NT, P, COLS),
        "tokens_r": tokens_r.reshape(NT, P, TS * D),
        "targets": targets.reshape(NT, 2, 4, NU // 2, 2, D).transpose(2, 1, 5, 3, 0, 4).reshape(P, NT * NU),
        "lens": np.tile(np.repeat(lens.reshape(NT, 2, 4, NU).transpose(3, 0, 2, 1).reshape(NU, NT * QJ), NI, axis=0), (NC, 1)),
        "heads": heads.reshape(2, 2, 32, 2, NT // 4, 2, D).transpose(0, 1, 5, 6, 3, 4, 2).reshape(P, 2 * 512),
        "params": params, "cbig": big, "chot": hot,
    }
    arrays = {k: np.ascontiguousarray(v) for k, v in arrays.items()}

    nc = bacc.Bacc("TRN2", target_bir_lowering=False, num_devices=1)
    args = [nc.dram_tensor(f"in_{k}", v.shape, mybir.dt.from_np(v.dtype), kind="ExternalInput").ap()
            for k, v in arrays.items()]
    y = nc.dram_tensor("y", (4, 512), F32, kind="ExternalOutput").ap()
    build(nc, *args, y)
    r = run_bass_kernel_spmd(nc, [{f"in_{k}": v for k, v in arrays.items()}], core_ids=[0])
    return r.results[0]["y"].reshape(2, 2, NT // 4, 32).transpose(2, 1, 0, 3).reshape(B, 1)
```

```python
from contextlib import ExitStack

import numpy as np

import concourse.bass as bass
from concourse import mybir

F32 = mybir.dt.float32
BF16 = mybir.dt.bfloat16
I32 = mybir.dt.int32
U16 = mybir.dt.uint16
ALU = mybir.AluOpType
ACT = mybir.ActivationFunctionType
AX_X = mybir.AxisListType.X

P = 128
B, L, D = 2048, 200, 16
AH1, AH2 = 16, 8
MH1, MH2 = 32, 16
TU = 64
NT = 2 * B // TU
NU, NI, NA = 8, 4, 2
NK = L // (NA * NI)
NC = 4
KC = -(-NK // NC)
K_OF = [0, KC, 2 * KC, NK - KC]
QJ = 8
UC = L
COLS = NU * UC
HC = COLS // 2
BC = 2 * UC
SC = KC * NU * NI
TS = NA * KC * QJ
RING = 3
UNROLL = 6
T_HEAD = [0, NT // 2 - 4, NT // 2]
T_SUMS = [0, T_HEAD[1] // 2, *T_HEAD[1:]]
PARTS = 3
CK = PARTS * NU

C_G8 = 0
C_POOL = C_G8 + 8
C_TOK = C_POOL + 4 * 32
C_Q4 = C_TOK + NA * KC
C_JT = C_Q4 + 4
C_W3 = C_JT + 4
C_END = C_W3 + 32
K_R1, K_R16 = 0, P
K_W16B = 2 * P
K_B1 = K_W16B + 4 * AH1 + AH2 + 2
K_EARLY = K_B1 + AH1
K_R8, K_R32, K_SEL = K_EARLY, K_EARLY + P, K_EARLY + 2 * P
K_ONE8 = K_SEL + 3 * P
K_W32 = K_ONE8 + P
K_W16A = K_W32 + MH2 + 2
K_W8 = K_W16A + 2
K_MW1 = K_W8 + 3
K_B3 = K_MW1 + MH1
K_END = K_B3 + 2
R_W1 = 0
R_W2 = R_W1 + 4 * AH1
R_W3M, R_MB2 = R_W2 + AH2, R_W2 + AH2 + 1
R_B1 = R_MB2 + 1
R_EARLY = R_B1 + AH1
R_MW2, R_MB1 = R_EARLY, R_EARLY + MH2
R_AL = R_MB1 + 1
R_B2, R_W3 = R_AL + 4, R_AL + 5
R_M1 = R_W3 + 1
R_B3, R_MB3 = R_M1 + 3 * MH1, R_M1 + 3 * MH1 + 1
R_END = R_MB3 + 1
A_M1, A_1, A_M2, A_2 = range(4)


def shape_constants():
    p = np.arange(P)
    big = np.zeros((P, C_END), np.float32)
    big[:, C_G8:C_G8 + 8] = p[:, None] // 16 == np.arange(8)
    for q in range(4):
        big[:, C_POOL + 32 * q:C_POOL + 32 * q + 32] = 8 * q + (p[:, None] // NI) % NU == np.arange(32)
    kk = np.arange(KC)
    for c in range(NC):
        double = K_OF[c] + kk < (K_OF[c - 1] + KC if c else 0)
        for i in range(NI):
            at = np.concatenate([np.where(double, 2.0 ** 31, L // NA * a + NI * (K_OF[c] + kk) + i) for a in range(NA)])
            big[p[(p // 32 == c) & (p % NI == i)], C_TOK:C_TOK + NA * KC] = at
    big[:, C_Q4:C_Q4 + 4] = p[:, None] // 32 == np.arange(4)
    big[:, C_JT:C_JT + 4] = 2 * (p[:, None] // 64) + (p[:, None] // 16) % 2 == np.arange(4)
    big[:, C_W3:] = p[:, None] // 8 == np.arange(32)
    rep = np.zeros((5 * D, K_END), np.float32)
    rep[:8, K_ONE8:K_ONE8 + P] = 1
    for at, width in ((K_R1, 1), (K_R8, 8), (K_R16, 16), (K_R32, 32)):
        rep[:width, at:at + P] = np.arange(width)[:, None] == p % width
    for p_ in range(P):
        h, f = (p_ // 32) % 2, p_ % 16
        rep[(2 * D if h else 0) + f, K_SEL + p_] = 1
        if h == 0:
            rep[4 * D + f, K_SEL + P + p_] = 1
        rep[(3 * D if h else D) + f, K_SEL + 2 * P + p_] = 1
    hot = np.zeros((CK, 4, BC), np.float32)
    for k in range(CK):
        u = 2 * (k % (NU // 2)) + k // (CK // 2)
        hot[k, u // 2, (u % 2) * UC:(u % 2 + 1) * UC] = 1
    hot_bits = hot.reshape(CK, -1).astype(np.uint16) * np.uint16(0x3F80)
    return big, rep, hot_bits


def build(nc, tokens_t, tokens_r, targets, lens, heads, params, cbig, chot, y_out):
    bias_dram = nc.dram_tensor("bias_parts", (NT, CK * P), BF16).ap()

    with ExitStack() as ctx:
        def sb(name, shape, dt=F32):
            return ctx.enter_context(nc.sbuf_tensor(name, shape, dt))

        def psum(name, shape):
            return ctx.enter_context(nc.psum_tensor(name, shape, F32))

        def sem(name):
            return ctx.enter_context(nc.semaphore(name))

        big = sb("big", [P, C_END])
        par = sb("par", [5 * D, K_END])
        hot = sb("hot", [CK, 4 * BC], BF16)
        R = sb("R", [P, R_END])
        beta = sb("beta", [P, 4])
        is_one = sb("is_one", [P, 4])
        ratio = sb("ratio", [P, 4])
        inv_beta = sb("inv_beta", [P, 4])
        oma = sb("oma", [P, 4])
        w3beta = sb("w3beta", [P, 1])
        w2beta = sb("w2beta", [P, AH2])
        w3ab = sb("w3ab", [8, 2])
        Ws = sb("Ws", [P, AH1])
        Wc = sb("Wc", [P, AH1])
        BDc = sb("BDc", [P, P])
        BD2 = sb("BD2", [P, 64])
        W3s = sb("W3s", [P, 32])
        M1 = sb("M1", [P, 3, P])
        M2 = sb("M2", [P, 64])
        M3 = sb("M3", [64, 4])
        tT = sb("tT", [P, NT * NU])
        lens_i = sb("lens_i", [P, NT * QJ], I32)
        LN = sb("LN", [P, NT * QJ])
        Cres = sb("Cres", [P, NU // 2 * P])
        C3 = sb("C3", [P, PARTS, NU // 2 * P], BF16)
        ZT = sb("ZT", [P, 2, 512])
        pooled = sb("pooled", [P, NT * QJ * D])
        pools = sb("pools", [P, 512])
        poolsT = sb("poolsT", [P, 512])
        X = sb("X", [P, RING, TS * D])
        XT = sb("XT", [P, RING, COLS])
        cb = sb("cb", [CK, RING, P], BF16)
        W1t = sb("W1t", [P, 2, P])
        W1c = sb("W1c", [P, 2, P])
        W1 = sb("W1", [P, 2, NU, P])
        G1 = sb("G1", [P, 2, 2 * BC])
        H1 = sb("H1", [P, 2, COLS])
        G2 = sb("G2", [P, 2, 2, BC])
        H2 = sb("H2", [P, 2, HC])
        SCb = sb("SCb", [P, 2, SC])
        SR = sb("SR", [P, 2, SC])
        MK = sb("MK", [P, NT * TS], I32)
        SM = sb("SM", [P, 2, TS])
        PR = sb("PR", [P, RING, NA * KC, QJ * D])
        g1, g2 = G1[:, 0, 0:512], G1[0:64, 1, 0:512]
        h1, h2 = H1[:, 0, 0:512], H1[0:64, 1, 0:512]
        yt = sb("yt", [4, 512])
        warm = sb("warm", [P, 1])

        x1 = psum("x1", [P, 4, 512])
        x2 = psum("x2", [P, 2, 512])
        sc = psum("sc", [P, 512])
        pp = psum("pp", [P, 512])

        early_in, params_in, targets_in, heads_in, big_in, hot_in, lens_in = (
            sem(n) for n in ("early_in", "params_in", "targets_in", "heads_in", "big_in", "hot_in", "lens_in"))
        x_in = [sem(f"x_in{r}") for r in range(RING)]
        xt_in = [sem(f"xt_in{r}") for r in range(RING)]
        first_cb = [sem(f"first_cb{r}") for r in range(RING)]
        cb_in = [sem(f"cb_in{r}") for r in range(RING)]
        rep_done, rep_ready, par_ready, w3ab_ready, m_ready = (
            sem(n) for n in ("rep_done", "rep_ready", "par_ready", "w3ab_ready", "m_ready"))
        dve_chain = sem("dve_chain")
        bdc_ready, c_done, c_split, c_stored, ln_ready, mk_diff, mk_done = (
            sem(n) for n in ("bdc_ready", "c_done", "c_split", "c_stored", "ln_ready", "mk_diff", "mk_done"))
        w_mul, w_add, w_ready, l1_done, silu1_ready, h1_ready = (
            sem(n) for n in ("w_mul", "w_add", "w_ready", "l1_done", "silu1_ready", "h1_ready"))
        l2_done, silu2_ready, h2_ready, l3_done, s_evac, st_done, sm_ready = (
            sem(n) for n in ("l2_done", "silu2_ready", "h2_ready", "l3_done", "s_evac", "st_done", "sm_ready"))
        prod_ready, fold_ready, pooled_done, last_prod = (
            sem(n) for n in ("prod_ready", "fold_ready", "pooled_done", "last_prod"))
        sum_done, pools_ready, pt_ready, y_ready, y_stored = (
            sem(n) for n in ("sum_done", "pools_ready", "pt_ready", "y_ready", "y_stored"))
        head_mm, head_sig, head_gate, head_h = (
            [sem(f"{name}{n}") for n in range(2)] for name in ("head_mm", "head_sig", "head_gate", "head_h"))
        head_x = [(x1[:, 0], x1[0:64, 1], x1[0:4, 2]), (x1[:, 3], x2[0:64, 0], x2[0:4, 1])]
        head_cols = [slice(lo * D, hi * D) for lo, hi in zip(T_HEAD, T_HEAD[1:])]

        positions = big[:, C_TOK:C_TOK + NA * KC]
        FIRST = -2
        LOOP0 = 6
        LOOPS = (NT - 2 - LOOP0) // UNROLL
        LOOP1 = LOOP0 + LOOPS * UNROLL

        def run_slots(eng, step, last):
            for s in range(FIRST, LOOP0):
                step(s, s)
            with eng.Fori(0, LOOPS) as n:
                for d in range(UNROLL):
                    step(n * UNROLL + (LOOP0 + d), LOOP0 + d, n)
            for s in range(LOOP1, last + 1):
                step(s, s)

        def tile(slot, known, rnd, lag):
            return rnd is not None or 0 <= known - lag < NT, slot - lag, known - lag

        def tiles_before(t, known, rnd, n):
            return rnd is not None or known >= n

        def loads(known, rnd):
            done = 16 * (known // RING + 1)
            return done if rnd is None else rnd * (16 * UNROLL // RING) + done

        block = ctx.enter_context(nc.Block())

        @block.sync
        def _(sp):
            def load_t(t, r):
                sp.dma_start(XT[:, r, :], tokens_t[bass.ds(t, 1), :, :].rearrange("o p c -> (o p) c")).then_inc(xt_in[r], 16)

            def load_r(t, r):
                sp.dma_start(X[:, r, :], tokens_r[bass.ds(t, 1), :, :].rearrange("o p c -> (o p) c")).then_inc(x_in[r], 16)

            def load_bias(t, r):
                sp.dma_start(cb[:, r, :], bias_dram[bass.ds(t, 1), :].rearrange("o (k m) -> (o k) m", m=P)
                             ).then_inc(cb_in[r], 16)

            sp.dma_start(tT[:], targets).then_inc(targets_in, 16)
            sp.dma_start(lens_i[:], lens).then_inc(lens_in, 16)
            for t in range(2):
                load_t(t, t)
            sp.wait_ge(c_split, PARTS)
            for t in range(RING):
                for u in range(2):
                    sp.dma_start(cb[u * CK // 2:(u + 1) * CK // 2, t, :],
                                 C3[2 * t + u:2 * t + u + 1].rearrange("p a (v m) -> p (a v) m", m=P)
                                 ).then_inc(first_cb[t], 16)
            sp.dma_start(bias_dram.rearrange("t (v c) -> (t v) c", v=2), C3[:].rearrange("p a m -> p (a m)")
                         ).then_inc(c_stored, 16)
            load_t(2, 2)
            sp.wait_ge(c_stored, 16)


            def load(t, k):
                if k < NT:
                    sp.wait_ge(l1_done, 2 * t - (2 * RING - 2))
                    load_t(t, k % RING)
                    load_bias(t, k % RING)
                if k >= 2 * RING:
                    sp.wait_ge(prod_ready, t - (2 * RING - 1))
                load_r(t - RING, k % RING)

            rounds = (NT - 2 * RING) // RING
            for t in range(RING, 2 * RING):
                load(t, t)
                if t == RING:
                    sp.dma_start(ZT[:].rearrange("p n c -> p (n c)"), heads).then_inc(heads_in, 16)
            with sp.Fori(0, rounds) as n:
                for r in range(RING):
                    load(n * RING + (2 * RING + r), 2 * RING + r)
            for t in range(RING * (rounds + 2), NT + RING):
                load(t, t)
            for n in range(2):
                sp.wait_ge(y_ready, n + 1)
                sp.dma_start(y_out[:, head_cols[n]], yt[:, head_cols[n]]).then_inc(y_stored, 16)
            sp.wait_ge(y_stored, 32)

        @block.scalar
        def _(act):
            act.dma_start(par[:, 0:K_EARLY], params[:, 0:K_EARLY]).then_inc(early_in, 16)
            act.dma_start(big[:], cbig).then_inc(big_in, 16)
            act.dma_start(par[:, K_EARLY:], params[:, K_EARLY:]).then_inc(params_in, 16)
            act.dma_start(hot[:].bitcast(U16), chot).then_inc(hot_in, 16)
            act.wait_ge(big_in, 16)
            nc.scalar.activation(warm[:], big[:, 0:1], ACT.Silu)

            def expand(t, k, g):
                nc.scalar.activation(
                    W1[:, k % 2, :, g * AH1:(g + 1) * AH1],
                    W1c[:, k % 2, :].rearrange("p (u h) -> p u h", u=NU),
                    ACT.Identity, scale=big[:, C_G8 + g:C_G8 + g + 1]).then_inc(w_ready, 1)

            for t in range(2):
                act.wait_ge(w_add, t + 1)
                for g in range(8):
                    expand(t, t, g)
            act.wait_ge(rep_ready, 2)

            def step(slot, known, rnd=None):
                runs, t, k = tile(slot, known, rnd, 3)
                if runs:
                    act.wait_ge(l3_done, t + 1)
                    if tiles_before(t, k, rnd, 2):
                        act.wait_ge(st_done, t - 1)
                    nc.scalar.activation(SCb[:, k % 2, :], sc[:, 0:SC], ACT.Identity,
                                         bias=R[:, R_B3:R_B3 + 1]).then_inc(s_evac, 1)
                for a in range(2):
                    runs, t, k = tile(slot, known, rnd, 0)
                    if runs:
                        act.wait_ge(l1_done, 2 * t + (a + 1))
                        nc.scalar.activation(G1[:, a].rearrange("p (b c) -> p b c", b=2), x1[:, 2 * a:2 * a + 2, 0:BC],
                                             ACT.Silu).then_inc(silu1_ready, 1)
                    runs, t, k = tile(slot, known, rnd, -1)
                    if a == 0 and runs and (rnd is not None or k >= 2):
                        act.wait_ge(w_add, t + 1)
                        if tiles_before(t, k, rnd, 2):
                            act.wait_ge(l1_done, 2 * t - 2)
                        for g in range(8):
                            expand(t, k, g)
                runs, t, k = tile(slot, known, rnd, 1)
                if runs:
                    act.wait_ge(l2_done, t + 1)
                    if tiles_before(t, k, rnd, 2):
                        act.wait_ge(h2_ready, t - 1)
                    nc.scalar.activation(G2[:, k % 2], x2[:, :, 0:BC], ACT.Silu,
                                         bias=R[:, R_B2:R_B2 + 1]).then_inc(silu2_ready, 1)

            run_slots(act, step, NT + 2)

            def pools_out(n):
                act.wait_ge(sum_done, n + 2)
                nc.scalar.copy(pools[:, head_cols[n]], pp[:, head_cols[n]]).then_inc(pools_ready, 1)

            def gate(n, layer):
                c = head_cols[n]
                rows, g, al, at = ((P, g1, A_M1, R_MB1), (64, g2, A_M2, R_MB2))[layer]
                act.wait_ge(head_mm[n], layer + 1)
                nc.scalar.activation(g[:, c], head_x[n][layer][:, c], ACT.Sigmoid,
                                     bias=R[0:rows, at:at + 1]).then_inc(head_sig[n], 1)
                act.wait_ge(head_sig[n], layer + 1)
                nc.scalar.activation(g[:, c], g[:, c], ACT.Identity, bias=R[0:rows, R_AL + al:R_AL + al + 1],
                                     scale=oma[0:rows, al:al + 1]).then_inc(head_gate[n], 1)

            def result(n):
                c = head_cols[n]
                act.wait_ge(head_mm[n], 3)
                nc.scalar.activation(yt[:, c], head_x[n][2][:, c], ACT.Sigmoid,
                                     bias=R[0:4, R_MB3:R_MB3 + 1]).then_inc(y_ready, 1)

            pools_out(0)
            gate(0, 0)
            gate(0, 1)
            pools_out(1)
            gate(1, 0)
            result(0)
            gate(1, 1)
            result(1)

        @block.vector
        def _(dve):
            count = [0]

            def chain(ins):
                count[0] += 1
                ins.then_inc(dve_chain, 1)
                dve.wait_ge(dve_chain, count[0])

            def user_products(t, k):
                nc.vector.tensor_tensor(
                    W1t[:, k % 2, :].rearrange("p (v u h) -> p v u h", u=2, h=AH1),
                    R[:, R_W1 + 3 * AH1:R_W1 + 4 * AH1].unsqueeze(1).unsqueeze(1).to_broadcast([P, NU // 2, 2, AH1]),
                    tT[:].rearrange("p (v tu) -> p v tu", v=NU // 2)[:, :, bass.ds(t * 2, 2)].unsqueeze(3)
                    .to_broadcast([P, NU // 2, 2, AH1]),
                    ALU.mult).then_inc(w_mul, 1)

            def user_weights(t, k):
                dve.wait_ge(w_mul, t + 1)
                nc.vector.tensor_tensor(
                    W1c[:, k % 2, :].rearrange("p (u h) -> p u h", u=NU),
                    W1t[:, k % 2, :].rearrange("p (u h) -> p u h", u=NU),
                    Ws[:].unsqueeze(1).to_broadcast([P, NU, AH1]), ALU.add).then_inc(w_add, 1)

            dve.wait_ge(rep_done, 1)
            nc.vector.tensor_copy(R[:, 0:R_EARLY], x2[:, 0, 0:R_EARLY]).then_inc(rep_ready, 1)
            dve.wait_ge(rep_ready, 1)
            w1m = [R[:, R_W1 + m * AH1:R_W1 + (m + 1) * AH1] for m in range(4)]
            chain(nc.vector.tensor_tensor(Wc[:], w1m[0], w1m[2], ALU.add))
            dve.wait_ge(big_in, 16)
            nc.vector.tensor_tensor(BDc[:].rearrange("p (g h) -> p g h", g=8),
                                    big[:, C_G8:C_G8 + 8].unsqueeze(2).to_broadcast([P, 8, AH1]),
                                    Wc[:].unsqueeze(1).to_broadcast([P, 8, AH1]), ALU.mult).then_inc(bdc_ready, 1)
            chain(nc.vector.tensor_tensor(Ws[:], w1m[1], w1m[2], ALU.subtract))
            dve.wait_ge(targets_in, 16)
            for t in range(2):
                user_products(t, t)
            for t in range(2):
                user_weights(t, t)
            dve.wait_ge(lens_in, 16)
            nc.vector.tensor_copy(LN[:], lens_i[:]).then_inc(ln_ready, 1)
            dve.wait_ge(c_done, 1)
            chain(nc.vector.tensor_tensor(
                Cres[:].rearrange("p (s h) -> p s h", h=AH1), x1[:, 0, :].rearrange("p (s h) -> p s h", h=AH1),
                R[:, R_B1:R_B1 + AH1].unsqueeze(1).to_broadcast([P, 32, AH1]), ALU.add))
            for n in range(PARTS):
                nc.vector.tensor_copy(C3[:, n, :], Cres[:]).then_inc(c_split, 1)
                if n < PARTS - 1:
                    dve.wait_ge(c_split, n + 1)
                    chain(nc.vector.tensor_tensor(Cres[:], Cres[:], C3[:, n, :], ALU.subtract))
            dve.wait_ge(params_in, 16)
            w8 = par[0:8, K_W8:K_W8 + 3]
            chain(nc.vector.tensor_tensor(w3ab[:, 0:1], w8[:, 2:3], w8[:, 0:1], ALU.mult))
            nc.vector.tensor_tensor(w3ab[:, 1:2], w3ab[:, 0:1], w8[:, 1:2], ALU.mult).then_inc(w3ab_ready, 1)
            dve.wait_ge(rep_done, 2)
            nc.vector.tensor_copy(R[:, R_EARLY:R_END], x2[:, 1, R_EARLY:R_END]).then_inc(rep_ready, 1)
            dve.wait_ge(rep_ready, 2)
            alphas = R[:, R_AL:R_AL + 4]
            chain(nc.vector.tensor_scalar(oma[:], alphas, -1.0, 1.0, ALU.mult, ALU.add))
            chain(nc.vector.tensor_scalar(is_one[:], oma[:], 0.0, 2.0 ** -30, ALU.is_equal, ALU.mult))
            chain(nc.vector.tensor_tensor(beta[:], oma[:], is_one[:], ALU.add))
            chain(nc.vector.reciprocal(inv_beta[:], beta[:]))
            chain(nc.vector.tensor_tensor(ratio[:], alphas, inv_beta[:], ALU.mult))
            chain(nc.vector.tensor_scalar(w2beta[:], R[:, R_W2:R_W2 + AH2], beta[:, A_1:A_1 + 1], None, ALU.mult))
            nc.vector.tensor_tensor(BD2[:].rearrange("p (g h) -> p g h", g=8),
                                    big[:, C_G8:C_G8 + 8].unsqueeze(2).to_broadcast([P, 8, AH2]),
                                    w2beta[:].unsqueeze(1).to_broadcast([P, 8, AH2]),
                                    ALU.mult).then_inc(par_ready, 1)
            chain(nc.vector.tensor_scalar(w3beta[:], R[:, R_W3:R_W3 + 1], beta[:, A_2:A_2 + 1], None, ALU.mult))
            nc.vector.tensor_scalar(W3s[:], big[:, C_W3:C_END], w3beta[:, 0:1], None,
                                    ALU.mult).then_inc(par_ready, 1)

            def masks(n):
                span = slice(n * NT // 2 * TS, (n + 1) * NT // 2 * TS)
                dve.wait_ge(mk_diff, n + 1)
                nc.vector.tensor_scalar(MK[:, span], MK[:, span].bitcast(F32), 0.0, -1.0, ALU.is_lt,
                                        ALU.mult).then_inc(mk_done, 1)

            masks(0)

            def scores_back(t, k, rnd):
                dve.wait_ge(s_evac, t + 1)
                if tiles_before(t, k, rnd, 2):
                    dve.wait_ge(sm_ready, t - 1)
                nc.vector.transpose(SR[:, k % 2, :], SCb[:, k % 2, :]).then_inc(st_done, 1)

            def masked(t, k, rnd):
                if rnd is None and k == 0:
                    dve.wait_ge(mk_done, 2)
                dve.wait_ge(st_done, t + 1)
                if tiles_before(t, k, rnd, 2):
                    dve.wait_ge(prod_ready, t - 1)
                nc.vector.tensor_tensor(
                    SM[:, k % 2, :].bitcast(I32).rearrange("p (a k r) -> p a k r", a=NA, k=KC),
                    MK[:, bass.ds(t * TS, TS)].rearrange("p (a k r) -> p a k r", a=NA, k=KC),
                    SR[:, k % 2, :].bitcast(I32).rearrange("p (k b r) -> p b k r", k=KC, r=QJ)[:, 0:NA],
                    ALU.bitwise_and).then_inc(sm_ready, 1)

            def sum_tokens(t, k, folded):
                dve.wait_ge(fold_ready, folded)
                nc.vector.reduce_sum(pooled[:, bass.ds(t * (QJ * D), QJ * D)],
                                     PR[:, k % RING, 0:KC + 1].rearrange("p k c -> p c k"), AX_X).then_inc(pooled_done, 1)

            def dice1(t, k, rnd, a):
                dve.wait_ge(silu1_ready, 2 * t + (a + 1))
                if a == 0 and tiles_before(t, k, rnd, 2):
                    dve.wait_ge(l2_done, t - 1)
                nc.vector.scalar_tensor_tensor(
                    out=H1[:, k % 2, a * HC:(a + 1) * HC].rearrange("p (b c) -> p b c", b=2),
                    in0=x1[:, 2 * a:2 * a + 2, 0:BC], scalar=ratio[:, A_1:A_1 + 1],
                    in1=G1[:, a].rearrange("p (b c) -> p b c", b=2),
                    op0=ALU.mult, op1=ALU.add).then_inc(h1_ready, 1)

            def step(slot, known, rnd=None):
                runs, t, k = tile(slot, known, rnd, 3)
                if runs:
                    scores_back(t, k, rnd)
                runs, t, k = tile(slot, known, rnd, 0)
                if runs:
                    dice1(t, k, rnd, 0)
                runs, t, k = tile(slot, known, rnd, 3)
                if runs:
                    masked(t, k, rnd)
                next_runs, next_t, next_k = tile(slot, known, rnd, -2)
                next_runs = next_runs and (rnd is not None or next_k >= 2)
                if next_runs:
                    dve.wait_ge(w_ready, 8 * next_t - 8)
                    user_products(next_t, next_k)
                ending = rnd is None and known >= NT - 1
                sum_runs, sum_t, sum_k = tile(slot, known, rnd, 4)
                if sum_runs and not ending:
                    sum_tokens(sum_t, sum_k, sum_t + 1)
                if next_runs:
                    user_weights(next_t, next_k)
                if known == 0 and rnd is None:
                    masks(1)
                runs, t, k = tile(slot, known, rnd, 0)
                if runs:
                    dice1(t, k, rnd, 1)
                runs, t, k = tile(slot, known, rnd, 1)
                if runs:
                    dve.wait_ge(silu2_ready, t + 1)
                    if tiles_before(t, k, rnd, 2):
                        dve.wait_ge(l3_done, t - 1)
                    nc.vector.scalar_tensor_tensor(
                        out=H2[:, k % 2, :].rearrange("p (b c) -> p b c", b=2), in0=x2[:, :, 0:BC],
                        scalar=ratio[:, A_2:A_2 + 1], in1=G2[:, k % 2], op0=ALU.mult, op1=ALU.add).then_inc(h2_ready, 1)
                if sum_runs and ending:
                    sum_tokens(sum_t, sum_k, sum_t + 1)

            run_slots(dve, step, NT)

            def pools_transposed(n):
                dve.wait_ge(pools_ready, n + 1)
                nc.vector.transpose(poolsT[:, head_cols[n]], pools[:, head_cols[n]]).then_inc(pt_ready, 1)

            t = NT - 2
            scores_back(t, t, None)
            masked(t, t, None)
            scores_back(t + 1, t + 1, None)
            masked(t + 1, t + 1, None)
            dve.wait_ge(x_in[t % RING], loads(t, None))
            dve.wait_ge(sm_ready, t + 1)
            nc.vector.tensor_tensor(
                PR[:, t % RING].rearrange("p k (c f) -> p (k c) f", f=D),
                X[:, t % RING, :].rearrange("p (c f) -> p c f", f=D),
                SM[:, t % 2, :].unsqueeze(2).to_broadcast([P, TS, D]), ALU.mult).then_inc(last_prod, 1)
            pools_transposed(0)
            sum_tokens(t - 1, t - 1, t)

            def dice_head(n, layer):
                c = head_cols[n]
                rows, g, h, at = ((P, g1, h1, R_MB1), (64, g2, h2, R_MB2))[layer]
                dve.wait_ge(head_gate[n], layer + 1)
                nc.vector.scalar_tensor_tensor(out=h[:, c], in0=head_x[n][layer][:, c], scalar=R[0:rows, at:at + 1],
                                               in1=g[:, c], op0=ALU.add, op1=ALU.mult).then_inc(head_h[n], 1)

            dve.wait_ge(last_prod, 1)
            nc.vector.reduce_sum(pooled[:, t * QJ * D:(t + 1) * QJ * D],
                                 PR[:, t % RING].rearrange("p k c -> p c k"), AX_X).then_inc(pooled_done, 1)
            dice_head(0, 0)
            sum_tokens(NT - 1, NT - 1, NT - 1)
            dice_head(0, 1)
            pools_transposed(1)
            dice_head(1, 0)
            dice_head(1, 1)

        @block.gpsimd
        def _(pool):
            pool.wait_ge(big_in, 16)
            pool.wait_ge(ln_ready, 1)
            for n in range(2):
                span = slice(n * NT // 2 * TS, (n + 1) * NT // 2 * TS)
                nc.gpsimd.tensor_tensor(
                    MK[:, span].bitcast(F32).rearrange("p (t a r) -> p t a r", t=NT // 2, r=QJ),
                    positions.unsqueeze(1).unsqueeze(3).to_broadcast([P, NT // 2, NA * KC, QJ]),
                    LN[:, n * NT // 2 * QJ:(n + 1) * NT // 2 * QJ].rearrange("p (t r) -> p t r", r=QJ).unsqueeze(2)
                    .to_broadcast([P, NT // 2, NA * KC, QJ]), ALU.subtract).then_inc(mk_diff, 1)

            def weigh(t, k, rnd, done):
                pool.wait_ge(x_in[k % RING], loads(k, rnd))
                pool.wait_ge(sm_ready, t + 1)
                if tiles_before(t, k, rnd, RING):
                    pool.wait_ge(pooled_done, t - (RING - 1))
                nc.gpsimd.tensor_tensor(
                    PR[:, k % RING].rearrange("p k (c f) -> p (k c) f", f=D),
                    X[:, k % RING, :].rearrange("p (c f) -> p c f", f=D),
                    SM[:, k % 2, :].unsqueeze(2).to_broadcast([P, TS, D]), ALU.mult).then_inc(prod_ready, 1)
                pool.wait_ge(prod_ready, done)
                nc.gpsimd.tensor_tensor(PR[:, k % RING, 1:KC], PR[:, k % RING, 1:KC], PR[:, k % RING, KC + 1:],
                                        ALU.add).then_inc(fold_ready, 1)

            def step(slot, known, rnd=None):
                if known == 0 and rnd is None:
                    pool.wait_ge(rep_ready, 2)
                    for n in range(3):
                        nc.gpsimd.tensor_tensor(
                            M1[:, n, :].rearrange("p (c h) -> p c h", c=4),
                            R[:, R_M1 + n * MH1:R_M1 + (n + 1) * MH1].unsqueeze(1).to_broadcast([P, 4, MH1]),
                            big[:, C_JT:C_JT + 4].unsqueeze(2).to_broadcast([P, 4, MH1]), ALU.mult).then_inc(m_ready, 1)
                    nc.gpsimd.tensor_tensor(
                        M2[:].rearrange("p (c h) -> p c h", c=4),
                        R[:, R_MW2:R_MW2 + MH2].unsqueeze(1).to_broadcast([P, 4, MH2]),
                        big[:, C_Q4:C_Q4 + 4].unsqueeze(2).to_broadcast([P, 4, MH2]), ALU.mult).then_inc(m_ready, 1)
                    nc.gpsimd.tensor_scalar(M3[:], big[0:64, C_G8:C_G8 + 4], R[0:64, R_W3M:R_W3M + 1], None,
                                            ALU.mult).then_inc(m_ready, 1)
                runs, t, k = tile(slot, known, rnd, 3)
                if runs:
                    weigh(t, k, rnd, t + 1)

            run_slots(pool, step, NT)
            weigh(NT - 1, NT - 1, None, NT - 1)

        @block.tensor
        def _(pe):
            pe.wait_ge(early_in, 16)
            mm = nc.tensor.matmul

            def spread(bank, at, rows, which, lo, hi, **flags):
                return mm(x2[:, bank, at:at + hi - lo], par[0:rows, which:which + P], par[0:rows, lo:hi], **flags)

            whole = dict(start=True, stop=True)
            spread(0, R_W1, 16, K_R16, K_W16B, K_B1, **whole)
            spread(0, R_B1, 1, K_R1, K_B1, K_EARLY, **whole).then_inc(rep_done, 1)
            pe.wait_ge(targets_in, 16)
            pe.wait_ge(bdc_ready, 1)
            for v in range(NU // 2):
                last = mm(x1[:, 0, v * P:(v + 1) * P], tT[:, v * P:(v + 1) * P], BDc[:], **whole)
            last.then_inc(c_done, 1)
            pe.wait_ge(params_in, 16)
            spread(1, R_MW2, 32, K_R32, K_W32, K_W16A, **whole)
            spread(1, R_AL + 1, 16, K_R16, K_W16A, K_W8, **whole)
            spread(1, R_AL + 3, 8, K_R8, K_W8, K_MW1, **whole)
            for n in range(3):
                spread(1, R_M1 + n * MH1, 5 * D, K_SEL + n * P, K_MW1, K_MW1 + MH1, **whole)
            spread(1, R_B3, 1, K_R1, K_B3, K_B3 + 2, start=True, stop=False)
            pe.wait_ge(w3ab_ready, 1)
            mm(x2[:, 1, R_B3:R_B3 + 1], par[0:8, K_ONE8:K_ONE8 + P], w3ab[:, 1:2], start=False,
               stop=True).then_inc(rep_done, 1)
            pe.wait_ge(hot_in, 16)
            pe.wait_ge(c_split, 1)

            def pool_sums(n):
                lo, hi = T_SUMS[n:n + 2]
                pe.wait_ge(pooled_done, NT // 2 + hi)
                pv = pooled[:].rearrange("p (s t q j f) -> p s j q t f", s=2, q=4, j=2, f=D)
                for q in range(4):
                    for c in range(4):
                        last = mm(pp[32 * c:32 * c + 32, lo * D:hi * D].rearrange("p (t f) -> p t f", f=D),
                                  big[:, C_POOL + 32 * q:C_POOL + 32 * q + 32], pv[:, c % 2, c // 2, q, lo:hi],
                                  start=q == 0, stop=q == 3)
                last.then_inc(sum_done, 1)

            def step(slot, known, rnd=None):
                if rnd is None and known >= NT:
                    pool_sums(known - NT)
                runs, t, k = tile(slot, known, rnd, 0)
                if runs:
                    for a in range(2):
                        if a == 0:
                            if rnd is None and k < RING:
                                pe.wait_ge(first_cb[k], 32)
                            else:
                                pe.wait_ge(cb_in[k % RING], loads(k - RING, rnd))
                            pe.wait_ge(xt_in[k % RING], loads(k, rnd))
                            pe.wait_ge(w_ready, 8 * t + 8)
                        if tiles_before(t, k, rnd, 1):
                            pe.wait_ge(h1_ready, 2 * t + (a - 1))
                        for bank in (2 * a, 2 * a + 1):
                            mm(x1[:, bank, 0:BC], cb[:, k % RING, :], hot[:, bank * BC:(bank + 1) * BC],
                               start=True, stop=False)
                            for u in (2 * bank, 2 * bank + 1):
                                last = mm(x1[:, bank, (u % 2) * UC:(u % 2 + 1) * UC], W1[:, k % 2, u, :],
                                          XT[:, k % RING, u * UC:(u + 1) * UC], start=False, stop=u % 2 == 1)
                        last.then_inc(l1_done, 1)
                runs, t, k = tile(slot, known, rnd, 1)
                if runs:
                    if rnd is None and k == 0:
                        pe.wait_ge(par_ready, 1)
                    pe.wait_ge(h1_ready, 2 * t + 2)
                    if tiles_before(t, k, rnd, 1):
                        pe.wait_ge(h2_ready, t)
                    hv = H1[:, k % 2, :].rearrange("p (u c) -> p u c", u=NU)
                    for v in range(2):
                        for half in range(2):
                            last = mm(x2[64 * half:64 * half + 64, v, 0:BC].rearrange("p (u c) -> p u c", u=4), BD2[:],
                                      hv[:, 4 * v:4 * v + 4, half * UC // 2:(half + 1) * UC // 2], start=True, stop=True)
                    last.then_inc(l2_done, 1)
                runs, t, k = tile(slot, known, rnd, 2)
                if runs:
                    if rnd is None and k == 0:
                        pe.wait_ge(par_ready, 2)
                    pe.wait_ge(h2_ready, t + 1)
                    if tiles_before(t, k, rnd, 1):
                        pe.wait_ge(s_evac, t)
                    hv = H2[:, k % 2, :].rearrange("p (u k i) -> p k u i", u=NU, i=NI)
                    for c in range(NC):
                        last = mm(sc[32 * c:32 * c + 32, 0:SC].rearrange("p (k u i) -> p k u i", u=NU, i=NI), W3s[:],
                                  hv[:, K_OF[c]:K_OF[c] + KC], start=True, stop=True)
                    last.then_inc(l3_done, 1)

            run_slots(pe, step, NT + 1)
            pe.wait_ge(m_ready, 5)
            pe.wait_ge(heads_in, 16)
            pe.wait_ge(h1_ready, 2 * NT)

            def head1(n):
                c = head_cols[n]
                for m in range(2):
                    mm(head_x[n][0][:, c], M1[:, m, :], ZT[:, m, c], start=m == 0, stop=False)
                pe.wait_ge(pt_ready, n + 1)
                mm(head_x[n][0][:, c], M1[:, 2, :], poolsT[:, c], start=False, stop=True).then_inc(head_mm[n], 1)

            def head_next(n, layer):
                c = head_cols[n]
                weights, h = ((M2, h1), (M3, h2))[layer - 1]
                pe.wait_ge(head_h[n], layer)
                mm(head_x[n][layer][:, c], weights[:], h[:, c], start=True, stop=True).then_inc(head_mm[n], 1)

            head1(0)
            head_next(0, 1)
            pool_sums(2)
            head1(1)
            head_next(0, 2)
            head_next(1, 1)
            head_next(1, 2)


def kernel(**inputs):
    import concourse.bacc as bacc
    from concourse.bass_utils import run_bass_kernel_spmd

    a = {k.removeprefix("L0_rec_"): np.asarray(v) for k, v in inputs.items()}
    big, rep, hot = shape_constants()
    params = rep
    w1 = a["aW1"].reshape(4, D, AH1)

    def put(at, *columns):
        for c in columns:
            c = c.reshape(len(c), -1)
            params[:len(c), at:at + c.shape[1]] = c
            at += c.shape[1]

    put(K_W32, a["mW2"], a["mb1"], a["mal1"])
    put(K_W16A, a["aal1"], a["mal2"])
    put(K_W8, a["aal2"], a["ab2"], a["aW3"])
    put(K_W16B, *w1, a["aW2"], a["mW3"], a["mb2"])
    put(K_MW1, a["mW1"])
    put(K_B1, a["ab1"][None])
    put(K_B3, a["ab3"], a["mb3"])
    targets = np.concatenate([a["r_target1_emb"], a["r_target2_emb"]])
    lens = np.concatenate([a["r_seq1_len"], a["r_seq2_len"]])
    of_users = lens.reshape(NT, 2, 4, NU).transpose(3, 0, 2, 1).reshape(NU, NT * QJ)
    heads = np.zeros((2, 2, 32, 2, NT // 2, D), np.float32)
    of_tile = [v.reshape(NT // 2, 2, 32, D).transpose(1, 2, 0, 3)
               for v in (a["r_user_emb"], a["r_target1_emb"], a["r_target2_emb"])]
    heads[:, 0, :, 0], heads[:, 1, :, 0], heads[:, 0, :, 1] = of_tile
    tokens = np.concatenate([a["r_seq1_emb"], a["r_seq2_emb"]]).reshape(NT, 2, 4, NU, NA, NK, NI, D)
    tokens_r = np.zeros((NT, NC, NU, NI, NA, KC, 4, 2, D), np.float32)
    for c in range(NC):
        doubles = K_OF[c - 1] + KC - K_OF[c] if c else 0
        chunk = tokens[..., K_OF[c] + doubles:K_OF[c] + KC, :, :]
        tokens_r[:, c, :, :, :, doubles:] = chunk.transpose(0, 3, 6, 4, 5, 2, 1, 7)
    arrays = {
        "tokens_t": tokens.transpose(0, 2, 1, 7, 3, 4, 5, 6).reshape(NT, P, COLS),
        "tokens_r": tokens_r.reshape(NT, P, TS * D),
        "targets": targets.reshape(NT, 2, 4, NU // 2, 2, D).transpose(2, 1, 5, 3, 0, 4).reshape(P, NT * NU),
        "lens": np.tile(np.repeat(of_users, NI, axis=0), (NC, 1)),
        "heads": heads.reshape(2, 2, 32, 2, NT // 4, 2, D).transpose(0, 1, 5, 6, 3, 4, 2).reshape(P, 2 * 512),
        "params": params, "cbig": big, "chot": hot,
    }
    arrays = {k: np.ascontiguousarray(v) for k, v in arrays.items()}

    nc = bacc.Bacc("TRN2", target_bir_lowering=False, num_devices=1)
    args = [nc.dram_tensor(f"in_{k}", v.shape, mybir.dt.from_np(v.dtype), kind="ExternalInput").ap()
            for k, v in arrays.items()]
    y = nc.dram_tensor("y", (4, 512), F32, kind="ExternalOutput").ap()
    build(nc, *args, y)
    r = run_bass_kernel_spmd(nc, [{f"in_{k}": v for k, v in arrays.items()}], core_ids=[0])
    return r.results[0]["y"].reshape(2, 2, NT // 4, 32).transpose(2, 1, 0, 3).reshape(B, 1)
```
